# Optimizing a Trainium2 kernel written in Bass

```python
import numpy as np
import jax
import jax.numpy as jnp

def _softmax(x, axis=-1):
    return jax.nn.softmax(x, axis=axis)

def _gelu(x):
    return jax.nn.gelu(x, approximate=True)

def _silu(x):
    return jax.nn.silu(x)

def _sigmoid(x):
    return jax.nn.sigmoid(x)

def _layernorm(x, axis=-1, eps=1e-05):
    m = jnp.mean(x, axis=axis, keepdims=True)
    v = jnp.var(x, axis=axis, keepdims=True)
    return (x - m) / jnp.sqrt(v + eps)

def _scatter_add(tgt, idx, src, axis=0):
    return tgt.at[idx].add(src)

def _segment_sum(src, seg, n):
    return jax.ops.segment_sum(src, seg, n)
kernel_name = 'mk_hybrid_d1_jaxref_r8_079c1e'

def setup_inputs(seed: int=0):
    np.random.seed(seed)
    _w = jnp.asarray

    def _L0_attn_a_setup():
        import math
        import jax, jax.numpy as jnp
        import numpy as np
        B, L, D_MODEL = (4, 128, 128)
        EXPAND, D_STATE, D_CONV = (2, 16, 4)
        D_INNER = EXPAND * D_MODEL
        DT_RANK = int(math.ceil(D_MODEL / 16))

        def _mamba_residual(x, norm_w, in_proj_w, conv_w, conv_b, x_proj_w, dt_w, dt_b, A_log, Dp, out_proj_w, ff_w1, ff_b1, ff_w2, ff_b2, ff_ln_w, ff_ln_b):
            b, l, _ = x.shape
            xn = x * jax.lax.rsqrt(jnp.mean(x * x, -1, keepdims=True) + 1e-05) * norm_w
            u, res = jnp.split(xn @ in_proj_w.T, 2, axis=-1)
            up = jnp.concatenate([jnp.zeros((b, D_CONV - 1, D_INNER), x.dtype), u], axis=1)
            conv = sum((up[:, k:k + l, :] * conv_w[:, k] for k in range(D_CONV))) + conv_b
            u_c = jax.nn.silu(conv)
            dbl = u_c @ x_proj_w.T
            dt_r = dbl[..., :DT_RANK]
            Bm = dbl[..., DT_RANK:DT_RANK + D_STATE]
            Cm = dbl[..., DT_RANK + D_STATE:]
            delta = jax.nn.softplus(dt_r @ dt_w.T + dt_b)
            A = -jnp.exp(A_log)

            def step(h, t):
                u_t, d_t, B_t, C_t = t
                dA = jnp.exp(d_t[:, :, None] * A)
                h = dA * h + (d_t * u_t)[:, :, None] * B_t[:, None, :]
                y_t = jnp.einsum('bdn,bn->bd', h, C_t)
                return (h, y_t)
            h0 = jnp.zeros((b, D_INNER, D_STATE), x.dtype)
            xs = (u_c.transpose(1, 0, 2), delta.transpose(1, 0, 2), Bm.transpose(1, 0, 2), Cm.transpose(1, 0, 2))
            hT, ys = jax.lax.scan(step, h0, xs)
            y = ys.transpose(1, 0, 2) + u_c * Dp
            y = y * jax.nn.silu(res)
            out = y @ out_proj_w.T + x
            h1 = jax.nn.gelu(out @ ff_w1.T + ff_b1, approximate=False)
            z = h1 @ ff_w2.T + ff_b2 + out
            mu = jnp.mean(z, -1, keepdims=True)
            var = jnp.mean((z - mu) ** 2, -1, keepdims=True)
            out_f = (z - mu) * jax.lax.rsqrt(var + 1e-05) * ff_ln_w + ff_ln_b
            hidden = jnp.concatenate([hT.reshape(b, 1, -1), up[:, -(D_CONV - 1):, :].reshape(b, 1, -1)], axis=-1)
            return (out_f, hidden)

        def _reference_tuple_inner(x, norm_w, in_proj_w, conv_w, conv_b, x_proj_w, dt_w, dt_b, A_log, Dp, out_proj_w, ff_w1, ff_b1, ff_w2, ff_b2, ff_ln_w, ff_ln_b):
            return _mamba_residual(x, norm_w, in_proj_w, conv_w, conv_b, x_proj_w, dt_w, dt_b, A_log, Dp, out_proj_w, ff_w1, ff_b1, ff_w2, ff_b2, ff_ln_w, ff_ln_b)
        key = jax.random.key(seed)
        ks = jax.random.split(key, 12)
        rn = lambda k, shp, s: jax.random.normal(k, shp, jnp.float32) * s
        inp = {}
        inp['x'] = jax.random.normal(ks[0], (B, L, D_MODEL), jnp.float32)
        inp['norm_w'] = jnp.ones((D_MODEL,), jnp.float32)
        inp['in_proj_w'] = rn(ks[1], (2 * D_INNER, D_MODEL), 1.0 / math.sqrt(D_MODEL))
        inp['conv_w'] = rn(ks[2], (D_INNER, D_CONV), 1.0 / math.sqrt(D_CONV))
        inp['conv_b'] = jnp.zeros((D_INNER,), jnp.float32)
        inp['x_proj_w'] = rn(ks[3], (DT_RANK + 2 * D_STATE, D_INNER), 1.0 / math.sqrt(D_INNER))
        dt_std = DT_RANK ** (-0.5)
        inp['dt_w'] = jax.random.uniform(ks[4], (D_INNER, DT_RANK), jnp.float32, -dt_std, dt_std)
        dt = jnp.clip(jnp.exp(jax.random.uniform(ks[5], (D_INNER,), jnp.float32) * (math.log(0.1) - math.log(0.001)) + math.log(0.001)), 0.0001)
        inp['dt_b'] = dt + jnp.log(-jnp.expm1(-dt))
        inp['A_log'] = jnp.log(jnp.tile(jnp.arange(1, D_STATE + 1, dtype=jnp.float32)[None, :], (D_INNER, 1)))
        inp['Dp'] = jnp.ones((D_INNER,), jnp.float32)
        inp['out_proj_w'] = rn(ks[6], (D_MODEL, D_INNER), 1.0 / math.sqrt(D_INNER))
        inp['ff_w1'] = rn(ks[7], (D_MODEL, D_MODEL), 1.0 / math.sqrt(D_MODEL))
        inp['ff_b1'] = jnp.zeros((D_MODEL,), jnp.float32)
        inp['ff_w2'] = rn(ks[8], (D_MODEL, D_MODEL), 1.0 / math.sqrt(D_MODEL))
        inp['ff_b2'] = jnp.zeros((D_MODEL,), jnp.float32)
        inp['ff_ln_w'] = jnp.ones((D_MODEL,), jnp.float32)
        inp['ff_ln_b'] = jnp.zeros((D_MODEL,), jnp.float32)
        return inp
    _L0_attn_a_in = _L0_attn_a_setup()

    def _L0_attn_b_setup():
        import jax, jax.numpy as jnp
        import numpy as np
        B, T, H, S = (8, 512, 128, 16)
        LN_EPS = 1e-05

        def _forward(x, W_in, b_in, B_mat, C_mat, W_B, b_B, W_D, b_D, W_out, b_out, W_ig, b_ig, W_fg, b_fg, gamma, beta):
            xp = x @ W_in + b_in
            Bx = (xp @ W_B + b_B) @ B_mat
            ig = jax.nn.sigmoid(xp @ W_ig + b_ig)
            fg = jax.nn.sigmoid(xp @ W_fg + b_fg)

            def step(h, inp):
                fg_t, ig_t, bx_t = inp
                h = fg_t * h + ig_t * bx_t
                return (h, h)
            h0 = jnp.zeros((xp.shape[0], B_mat.shape[1]), xp.dtype)
            xs = (jnp.swapaxes(fg, 0, 1), jnp.swapaxes(ig, 0, 1), jnp.swapaxes(Bx, 0, 1))
            _, hs = jax.lax.scan(step, h0, xs)
            hs = jnp.swapaxes(hs, 0, 1)
            y = jnp.tanh(hs @ C_mat + (xp @ W_D + b_D))
            y = y @ W_out + b_out + xp
            mu = jnp.mean(y, axis=-1, keepdims=True)
            var = jnp.var(y, axis=-1, keepdims=True)
            y = (y - mu) * jax.lax.rsqrt(var + LN_EPS) * gamma + beta
            return y
        key = jax.random.key(seed)
        ks = jax.random.split(key, 16)
        inv_h = 1.0 / np.sqrt(H)
        d = {'x': jax.random.normal(ks[0], (B, T, H), jnp.float32), 'W_in': jax.random.normal(ks[1], (H, H), jnp.float32) * inv_h, 'b_in': jnp.zeros((H,), jnp.float32), 'B_mat': jax.random.normal(ks[2], (H, S), jnp.float32) * 0.1, 'C_mat': jax.random.normal(ks[3], (S, H), jnp.float32) * 0.1, 'W_B': jax.random.normal(ks[4], (H, H), jnp.float32) * inv_h, 'b_B': jnp.zeros((H,), jnp.float32), 'W_D': jax.random.normal(ks[5], (H, H), jnp.float32) * inv_h, 'b_D': jnp.zeros((H,), jnp.float32), 'W_out': jax.random.normal(ks[6], (H, H), jnp.float32) * inv_h, 'b_out': jnp.zeros((H,), jnp.float32), 'W_ig': jax.random.normal(ks[7], (H, S), jnp.float32) * inv_h, 'b_ig': jnp.zeros((S,), jnp.float32), 'W_fg': jax.random.normal(ks[8], (H, S), jnp.float32) * inv_h, 'b_fg': jnp.zeros((S,), jnp.float32), 'gamma': jnp.ones((H,), jnp.float32), 'beta': jnp.zeros((H,), jnp.float32)}
        return d
    _L0_attn_b_in = _L0_attn_b_setup()

    def _L0_ffn_setup():
        import jax, jax.numpy as jnp
        import numpy as np
        DIM = 128
        HEADS = 8
        NUM_EXPERTS = 8192
        NUM_KEYS = 32
        DIM_KEY = 64
        PK_TOPK = 16
        FINAL_TOPK = 1
        BATCH, SEQ = (4, 256)
        key = jax.random.key(seed)
        k1, k2, k3, k4, k5 = jax.random.split(key, 5)
        x = jax.random.normal(k1, (BATCH, SEQ, DIM), jnp.float32)
        w_q = jax.random.normal(k2, (DIM, 2 * HEADS * DIM_KEY), jnp.float32) * 0.02
        keys = jax.random.normal(k3, (HEADS, NUM_KEYS, 2, DIM_KEY), jnp.float32) * 0.02
        w_down = jax.random.normal(k4, (NUM_EXPERTS, DIM), jnp.float32) * 0.02
        w_up = jax.random.normal(k5, (NUM_EXPERTS, DIM), jnp.float32) * 0.02
        return {'x': x, 'w_q': w_q, 'keys': keys, 'w_down': w_down, 'w_up': w_up}
    _L0_ffn_in = _L0_ffn_setup()
    _d = {'L0_attn_a_x': _L0_attn_a_in['x'], 'L0_attn_a_norm_w': _L0_attn_a_in['norm_w'], 'L0_attn_a_in_proj_w': _L0_attn_a_in['in_proj_w'], 'L0_attn_a_conv_w': _L0_attn_a_in['conv_w'], 'L0_attn_a_conv_b': _L0_attn_a_in['conv_b'], 'L0_attn_a_x_proj_w': _L0_attn_a_in['x_proj_w'], 'L0_attn_a_dt_w': _L0_attn_a_in['dt_w'], 'L0_attn_a_dt_b': _L0_attn_a_in['dt_b'], 'L0_attn_a_A_log': _L0_attn_a_in['A_log'], 'L0_attn_a_Dp': _L0_attn_a_in['Dp'], 'L0_attn_a_out_proj_w': _L0_attn_a_in['out_proj_w'], 'L0_attn_a_ff_w1': _L0_attn_a_in['ff_w1'], 'L0_attn_a_ff_b1': _L0_attn_a_in['ff_b1'], 'L0_attn_a_ff_w2': _L0_attn_a_in['ff_w2'], 'L0_attn_a_ff_b2': _L0_attn_a_in['ff_b2'], 'L0_attn_a_ff_ln_w': _L0_attn_a_in['ff_ln_w'], 'L0_attn_a_ff_ln_b': _L0_attn_a_in['ff_ln_b'], 'L0_attn_b_W_in': _L0_attn_b_in['W_in'], 'L0_attn_b_b_in': _L0_attn_b_in['b_in'], 'L0_attn_b_B_mat': _L0_attn_b_in['B_mat'], 'L0_attn_b_C_mat': _L0_attn_b_in['C_mat'], 'L0_attn_b_W_B': _L0_attn_b_in['W_B'], 'L0_attn_b_b_B': _L0_attn_b_in['b_B'], 'L0_attn_b_W_D': _L0_attn_b_in['W_D'], 'L0_attn_b_b_D': _L0_attn_b_in['b_D'], 'L0_attn_b_W_out': _L0_attn_b_in['W_out'], 'L0_attn_b_b_out': _L0_attn_b_in['b_out'], 'L0_attn_b_W_ig': _L0_attn_b_in['W_ig'], 'L0_attn_b_b_ig': _L0_attn_b_in['b_ig'], 'L0_attn_b_W_fg': _L0_attn_b_in['W_fg'], 'L0_attn_b_b_fg': _L0_attn_b_in['b_fg'], 'L0_attn_b_gamma': _L0_attn_b_in['gamma'], 'L0_attn_b_beta': _L0_attn_b_in['beta'], 'L0_ffn_w_q': _L0_ffn_in['w_q'], 'L0_ffn_keys': _L0_ffn_in['keys'], 'L0_ffn_w_down': _L0_ffn_in['w_down'], 'L0_ffn_w_up': _L0_ffn_in['w_up']}
    _x0 = _d['L0_attn_a_x']
    _d['L0_attn_a_x'] = jax.random.normal(jax.random.fold_in(jax.random.key(seed), 1), (16, 512, 128), dtype=_x0.dtype)
    del _x0
    return _d

def reference(L0_attn_a_x, L0_attn_a_norm_w, L0_attn_a_in_proj_w, L0_attn_a_conv_w, L0_attn_a_conv_b, L0_attn_a_x_proj_w, L0_attn_a_dt_w, L0_attn_a_dt_b, L0_attn_a_A_log, L0_attn_a_Dp, L0_attn_a_out_proj_w, L0_attn_a_ff_w1, L0_attn_a_ff_b1, L0_attn_a_ff_w2, L0_attn_a_ff_b2, L0_attn_a_ff_ln_w, L0_attn_a_ff_ln_b, L0_attn_b_W_in, L0_attn_b_b_in, L0_attn_b_B_mat, L0_attn_b_C_mat, L0_attn_b_W_B, L0_attn_b_b_B, L0_attn_b_W_D, L0_attn_b_b_D, L0_attn_b_W_out, L0_attn_b_b_out, L0_attn_b_W_ig, L0_attn_b_b_ig, L0_attn_b_W_fg, L0_attn_b_b_fg, L0_attn_b_gamma, L0_attn_b_beta, L0_ffn_w_q, L0_ffn_keys, L0_ffn_w_down, L0_ffn_w_up):

    def _L0_attn_a_ref(x, norm_w, in_proj_w, conv_w, conv_b, x_proj_w, dt_w, dt_b, A_log, Dp, out_proj_w, ff_w1, ff_b1, ff_w2, ff_b2, ff_ln_w, ff_ln_b):
        import math
        import jax, jax.numpy as jnp
        import numpy as np
        B, L, D_MODEL = (4, 128, 128)
        EXPAND, D_STATE, D_CONV = (2, 16, 4)
        D_INNER = EXPAND * D_MODEL
        DT_RANK = int(math.ceil(D_MODEL / 16))

        def _mamba_residual(x, norm_w, in_proj_w, conv_w, conv_b, x_proj_w, dt_w, dt_b, A_log, Dp, out_proj_w, ff_w1, ff_b1, ff_w2, ff_b2, ff_ln_w, ff_ln_b):
            b, l, _ = x.shape
            xn = x * jax.lax.rsqrt(jnp.mean(x * x, -1, keepdims=True) + 1e-05) * norm_w
            u, res = jnp.split(xn @ in_proj_w.T, 2, axis=-1)
            up = jnp.concatenate([jnp.zeros((b, D_CONV - 1, D_INNER), x.dtype), u], axis=1)
            conv = sum((up[:, k:k + l, :] * conv_w[:, k] for k in range(D_CONV))) + conv_b
            u_c = jax.nn.silu(conv)
            dbl = u_c @ x_proj_w.T
            dt_r = dbl[..., :DT_RANK]
            Bm = dbl[..., DT_RANK:DT_RANK + D_STATE]
            Cm = dbl[..., DT_RANK + D_STATE:]
            delta = jax.nn.softplus(dt_r @ dt_w.T + dt_b)
            A = -jnp.exp(A_log)

            def step(h, t):
                u_t, d_t, B_t, C_t = t
                dA = jnp.exp(d_t[:, :, None] * A)
                h = dA * h + (d_t * u_t)[:, :, None] * B_t[:, None, :]
                y_t = jnp.einsum('bdn,bn->bd', h, C_t)
                return (h, y_t)
            h0 = jnp.zeros((b, D_INNER, D_STATE), x.dtype)
            xs = (u_c.transpose(1, 0, 2), delta.transpose(1, 0, 2), Bm.transpose(1, 0, 2), Cm.transpose(1, 0, 2))
            hT, ys = jax.lax.scan(step, h0, xs)
            y = ys.transpose(1, 0, 2) + u_c * Dp
            y = y * jax.nn.silu(res)
            out = y @ out_proj_w.T + x
            h1 = jax.nn.gelu(out @ ff_w1.T + ff_b1, approximate=False)
            z = h1 @ ff_w2.T + ff_b2 + out
            mu = jnp.mean(z, -1, keepdims=True)
            var = jnp.mean((z - mu) ** 2, -1, keepdims=True)
            out_f = (z - mu) * jax.lax.rsqrt(var + 1e-05) * ff_ln_w + ff_ln_b
            hidden = jnp.concatenate([hT.reshape(b, 1, -1), up[:, -(D_CONV - 1):, :].reshape(b, 1, -1)], axis=-1)
            return (out_f, hidden)

        def _reference_tuple_inner(x, norm_w, in_proj_w, conv_w, conv_b, x_proj_w, dt_w, dt_b, A_log, Dp, out_proj_w, ff_w1, ff_b1, ff_w2, ff_b2, ff_ln_w, ff_ln_b):
            return _mamba_residual(x, norm_w, in_proj_w, conv_w, conv_b, x_proj_w, dt_w, dt_b, A_log, Dp, out_proj_w, ff_w1, ff_b1, ff_w2, ff_b2, ff_ln_w, ff_ln_b)
        return _reference_tuple_inner(x, norm_w, in_proj_w, conv_w, conv_b, x_proj_w, dt_w, dt_b, A_log, Dp, out_proj_w, ff_w1, ff_b1, ff_w2, ff_b2, ff_ln_w, ff_ln_b)[0]

    def _L0_attn_b_ref(x, W_in, b_in, B_mat, C_mat, W_B, b_B, W_D, b_D, W_out, b_out, W_ig, b_ig, W_fg, b_fg, gamma, beta):
        import jax, jax.numpy as jnp
        import numpy as np
        B, T, H, S = (8, 512, 128, 16)
        LN_EPS = 1e-05

        def _forward(x, W_in, b_in, B_mat, C_mat, W_B, b_B, W_D, b_D, W_out, b_out, W_ig, b_ig, W_fg, b_fg, gamma, beta):
            xp = x @ W_in + b_in
            Bx = (xp @ W_B + b_B) @ B_mat
            ig = jax.nn.sigmoid(xp @ W_ig + b_ig)
            fg = jax.nn.sigmoid(xp @ W_fg + b_fg)

            def step(h, inp):
                fg_t, ig_t, bx_t = inp
                h = fg_t * h + ig_t * bx_t
                return (h, h)
            h0 = jnp.zeros((xp.shape[0], B_mat.shape[1]), xp.dtype)
            xs = (jnp.swapaxes(fg, 0, 1), jnp.swapaxes(ig, 0, 1), jnp.swapaxes(Bx, 0, 1))
            _, hs = jax.lax.scan(step, h0, xs)
            hs = jnp.swapaxes(hs, 0, 1)
            y = jnp.tanh(hs @ C_mat + (xp @ W_D + b_D))
            y = y @ W_out + b_out + xp
            mu = jnp.mean(y, axis=-1, keepdims=True)
            var = jnp.var(y, axis=-1, keepdims=True)
            y = (y - mu) * jax.lax.rsqrt(var + LN_EPS) * gamma + beta
            return y
        return _forward(x, W_in, b_in, B_mat, C_mat, W_B, b_B, W_D, b_D, W_out, b_out, W_ig, b_ig, W_fg, b_fg, gamma, beta)

    def _L0_ffn_ref(x, w_q, keys, w_down, w_up):
        import jax, jax.numpy as jnp
        import numpy as np
        DIM = 128
        HEADS = 8
        NUM_EXPERTS = 8192
        NUM_KEYS = 32
        DIM_KEY = 64
        PK_TOPK = 16
        FINAL_TOPK = 1
        BATCH, SEQ = (4, 256)
        b, n, d = x.shape
        q = (x @ w_q).reshape(b, n, 2, HEADS, DIM_KEY).transpose(2, 0, 1, 3, 4)
        sim = jnp.einsum('pbnhd,hkpd->pbnhk', q, keys)
        vals, idx = jax.lax.top_k(sim, PK_TOPK)
        sx, sy = (vals[0], vals[1])
        ix, iy = (idx[0], idx[1])
        all_scores = (sx[..., :, None] + sy[..., None, :]).reshape(b, n, HEADS, PK_TOPK * PK_TOPK)
        all_indices = (ix[..., :, None] * NUM_KEYS + iy[..., None, :]).reshape(b, n, HEADS, PK_TOPK * PK_TOPK)
        scores, pk_indices = jax.lax.top_k(all_scores, FINAL_TOPK)
        indices = jnp.take_along_axis(all_indices, pk_indices, axis=-1)
        weights_down = w_down[indices]
        weights_up = w_up[indices]
        h = jnp.einsum('bnd,bnhkd->bnhk', x, weights_down)
        h = jax.nn.gelu(h, approximate=False)
        h = h * jax.nn.relu(scores)
        return jnp.einsum('bnhk,bnhkd->bnd', h, weights_up)
    x = L0_attn_a_x
    x = x + _L0_attn_a_ref(_layernorm(x, axis=-1), L0_attn_a_norm_w, L0_attn_a_in_proj_w, L0_attn_a_conv_w, L0_attn_a_conv_b, L0_attn_a_x_proj_w, L0_attn_a_dt_w, L0_attn_a_dt_b, L0_attn_a_A_log, L0_attn_a_Dp, L0_attn_a_out_proj_w, L0_attn_a_ff_w1, L0_attn_a_ff_b1, L0_attn_a_ff_w2, L0_attn_a_ff_b2, L0_attn_a_ff_ln_w, L0_attn_a_ff_ln_b)
    x = x + _L0_ffn_ref(_layernorm(x, axis=-1), L0_ffn_w_q, L0_ffn_keys, L0_ffn_w_down, L0_ffn_w_up)
    x = x + _L0_attn_b_ref(_layernorm(x, axis=-1), L0_attn_b_W_in, L0_attn_b_b_in, L0_attn_b_B_mat, L0_attn_b_C_mat, L0_attn_b_W_B, L0_attn_b_b_B, L0_attn_b_W_D, L0_attn_b_b_D, L0_attn_b_W_out, L0_attn_b_b_out, L0_attn_b_W_ig, L0_attn_b_b_ig, L0_attn_b_W_fg, L0_attn_b_b_fg, L0_attn_b_gamma, L0_attn_b_beta)
    x = x + _L0_ffn_ref(_layernorm(x, axis=-1), L0_ffn_w_q, L0_ffn_keys, L0_ffn_w_down, L0_ffn_w_up)
    return x

_drawn_inputs = setup_inputs


def setup_inputs(seed=0):
    import zlib

    import numpy as np

    out = dict(_drawn_inputs(seed))
    spreads = {'L0_attn_a_norm_w': (1.0, 0.2),
     'L0_attn_a_conv_b': (0.0, 0.428),
     'L0_attn_a_Dp': (1.0, 0.2),
     'L0_attn_a_ff_b1': (0.0, 0.1),
     'L0_attn_a_ff_b2': (0.0, 0.1),
     'L0_attn_a_ff_ln_w': (1.0, 0.2),
     'L0_attn_a_ff_ln_b': (0.0, 0.1),
     'L0_attn_b_b_in': (0.0, 0.1),
     'L0_attn_b_b_B': (0.0, 0.514),
     'L0_attn_b_b_D': (0.0, 0.328),
     'L0_attn_b_b_out': (0.0, 0.1),
     'L0_attn_b_b_ig': (0.0, 0.8),
     'L0_attn_b_b_fg': (0.0, 0.8),
     'L0_attn_b_gamma': (1.0, 0.2),
     'L0_attn_b_beta': (0.0, 0.1)}
    factors = {'L0_attn_a_dt_w': 6.562,
     'L0_attn_a_dt_b': 3.735,
     'L0_attn_b_W_fg': 3.117,
     'L0_ffn_w_q': 8.0,
     'L0_ffn_keys': 8.0,
     'L0_ffn_w_down': 8.0,
     'L0_ffn_w_up': 8.0}
    for name, (base, spread) in spreads.items():
        noise = np.random.default_rng([zlib.crc32(name.encode()), seed]).standard_normal(out[name].shape)
        drawn = base * np.exp(spread * noise) if base else spread * noise
        out[name] = jnp.asarray(drawn.astype(out[name].dtype))
    for name, factor in factors.items():
        out[name] = (out[name] * factor).astype(out[name].dtype)
    return out
```

```python
from contextlib import ExitStack

import concourse.bass as bass
from concourse import mybir

ALU = mybir.AluOpType
ACT = mybir.ActivationFunctionType
F32 = mybir.dt.float32
BF16 = mybir.dt.bfloat16
I32 = mybir.dt.int32
U32 = mybir.dt.uint32
AX_X = mybir.AxisListType.X

P = 128
NB, T = 16, 512
NT = T // P
DI = 256
NH = DI // P
NS = 16
NK = 4
DR = 8
HEADS, KEYS, DK = 8, 32, 64
GR = 2 * HEADS
SIM = GR * KEYS
EPS = 1e-5

BC = 2 * NS
PART = (0, 64, 96)
DT0 = 32
IG, FG, BX = 0, 32, 64

NDA = 4
NP = 2
LEAD = 3

PRE, CORE, PA, PB, PC = "pre", "core", "A", "B", "C"
OFFSET = {PRE: 1, CORE: 0, PA: -1, PB: -2, PC: -3}
LAST_ITERATION = NB - 1 + 3
LOOP_FROM, LOOP_TO = 4, 14


def at(b, per, k=0):
    return b * per + (k + 1)


def later(b):
    return not (isinstance(b, int) and b == 0)


def second(b):
    return not (isinstance(b, int) and b < 2)


def phases(i):
    return {p for p, o in OFFSET.items() if 0 <= i + o < NB}


def run_pipeline(eng, iteration):
    iteration(-1, 1, phases(-1))
    for i in range(LOOP_FROM):
        iteration(i, i % 2, phases(i))
    every = set(OFFSET)
    with eng.Fori(LOOP_FROM, LOOP_TO, 2) as i:
        iteration(i, 0, every)
        iteration(i + 1, 1, every)
    for i in range(LOOP_TO, LAST_ITERATION + 1):
        iteration(i, i % 2, phases(i))


def build(nc, A):
    with ExitStack() as ctx:
        def sb(name, shape, dt=F32):
            return ctx.enter_context(nc.sbuf_tensor(name, shape, dt))

        def sem(name):
            return ctx.enter_context(nc.semaphore(name))

        ident = sb("ident", [P, P])
        pick = sb("pick", [P, BC], BF16)
        w_taps = sb("w_taps", [P, NK, DI])
        w_res = sb("w_res", [P, DI])
        w_xproj = sb("w_xproj", [P, NH, P])
        w_dt = sb("w_dt", [P, DI])
        w_out = sb("w_out", [P, NH, P])
        w_ff1 = sb("w_ff1", [P, P])
        w_ff2 = sb("w_ff2", [P, P])
        w_xp = sb("w_xp", [P, P])
        w_gate = sb("w_gate", [P, P])
        w_c = sb("w_c", [P, P])
        w_d = sb("w_d", [P, P])
        w_y = sb("w_y", [P, P])
        w_sim = sb("w_sim", [P, SIM])
        ln_w = sb("ln_w", [P, P])
        ln_b = sb("ln_b", [P, P])
        gamma = sb("gamma", [P, P])
        beta = sb("beta", [P, P])
        rank_rev = sb("rank_rev", [P, SIM], BF16)
        decay = sb("decay", [P, NH, NS])
        norm_w = sb("norm_w", [P, 1])
        conv_b = sb("conv_b", [P, NH])
        dt_b = sb("dt_b", [P, NH])
        d_skip = sb("d_skip", [P, NH])
        b_ff1 = sb("b_ff1", [P, 1])
        b_ff2 = sb("b_ff2", [P, 1])
        b_xp = sb("b_xp", [P, 1])
        b_y = sb("b_y", [P, 1])
        b_xpy = sb("b_xpy", [P, 1])
        b_d = sb("b_d", [P, 1])
        b_gate = sb("b_gate", [P, 1])
        b_wb = sb("b_wb", [P, 1])
        b_bx = sb("b_bx", [P, 1])
        b_mat = sb("b_mat", [P, NS])
        eps = sb("eps", [P, 1])
        idle_dve = sb("idle_dve", [P, 1])

        x_in = sb("x_in", [P, NT, P])
        xn0 = [sb(f"xn0_{q}", [P, NT, P]) for q in range(2)]
        xr = sb("xr", [P, NT, P])
        xrT = sb("xrT", [P, NK - 1 + T])
        ucs = [sb(f"ucs{q}", [P, 2 * NH, T]) for q in range(2)]
        dbl = sb("dbl", [P, T])
        split = [sb(f"split{q}", [P, T], BF16) for q in range(2)]
        rest = sb("rest", [P, T])
        soft = sb("soft", [P, NH, T])
        delta = [sb(f"delta{q}", [P, NH, T]) for q in range(2)]
        du = [sb(f"du{q}", [P, NH, T]) for q in range(2)]
        st0, mv0 = sb("st0", [P, NT, 6]), sb("mv0", [P, NT, 2])
        ln0, rs0, m20, rr0, s20 = (sb(n, [P, NT]) for n in ("ln0", "rs0", "m20", "rr0", "s20"))

        dA = sb("dA", [P, NDA, NH, T])
        hp = sb("hp", [P, NP, NH, T])

        outT, outTb, h1T, x_res = (sb(n, [P, T]) for n in ("outT", "outTb", "h1T", "x_res"))
        stA, mvA, lnA, rsA = sb("stA", [P, NT, 6]), sb("mvA", [P, NT, 2]), sb("lnA", [P, NT]), sb("rsA", [P, NT])
        stB, mvB, lnB, rsB = sb("stB", [P, NT, 6]), sb("mvB", [P, NT, 2]), sb("lnB", [P, NT]), sb("rsB", [P, NT])
        x1, x2, x3 = (sb(n, [P, NT, P]) for n in ("x1", "x2", "x3"))
        xnb = sb("xnb", [P, NT, P])
        xnbT = sb("xnbT", [P, T])
        xpT, xpTb, gates, hs = (sb(n, [P, T]) for n in ("xpT", "xpTb", "gates", "hs"))

        class Experts:

            def __init__(self, n):
                self.xn = sb(f"xn{n}", [P, NT, P])
                self.xnT = sb(f"xnT{n}", [P, T])
                self.mask = sb(f"mask{n}", [P, NT, SIM], BF16)
                self.rows = sb(f"rows{n}", [P, NT, HEADS, 2 * P])
                self.st, self.mv = sb(f"st{n}", [P, NT, 6]), sb(f"mv{n}", [P, NT, 2])
                self.ln, self.rs = sb(f"ln{n}", [P, NT]), sb(f"rs{n}", [P, NT])
                self.top = sb(f"top{n}", [P, NT, GR])
                self.rank = sb(f"rank{n}", [P, NT, GR])
                self.code = sb(f"code{n}", [P, NT, HEADS])
                self.score = sb(f"score{n}", [P, NT, HEADS])
                self.index = sb(f"index{n}", [P, NT, HEADS], U32)
                self.dot = sb(f"dot{n}", [P, NT, HEADS])
                self.act = sb(f"act{n}", [P, NT, HEADS])
                self.coef = sb(f"coef{n}", [P, NT, HEADS])
                self.mark = sb(f"mark{n}", [P, 1])
                self.started = sem(f"e{n}_started")
                self.stats = sem(f"e{n}_stats")
                self.logged = sem(f"e{n}_logged")
                self.rstd = sem(f"e{n}_rstd")
                self.normed = sem(f"e{n}_normed")
                self.turned = sem(f"e{n}_turned")
                self.turned_sb = sem(f"e{n}_turned_sb")
                self.sim = sem(f"e{n}_sim")
                self.topped = sem(f"e{n}_topped")
                self.masked = sem(f"e{n}_masked")
                self.picks = sem(f"e{n}_picks")
                self.indexed = sem(f"e{n}_indexed")
                self.fetched = [sem(f"e{n}_fetched{t}") for t in range(NT)]
                self.dotted = sem(f"e{n}_dotted")
                self.gelu = sem(f"e{n}_gelu")
                self.weighed = sem(f"e{n}_weighed")
                self.scaled = sem(f"e{n}_scaled")
                self.summed = sem(f"e{n}_summed")
                self.added = sem(f"e{n}_added")

        e1, e2 = Experts(1), Experts(2)

        bcast = [ctx.enter_context(nc.psum_tensor(f"bcast{k}", [P, 2, T], F32)) for k in range(2)]
        ysum = ctx.enter_context(nc.psum_tensor("ysum", [P, NH, T], F32))
        bank = [ctx.enter_context(nc.psum_tensor(f"bank{k}", [P, T], F32)) for k in range(2)]

        weights_in = sem("weights_in")
        cleared = sem("cleared")
        made = sem("made")
        folded = sem("folded")
        x_loaded = sem("x_loaded")
        p_stats = sem("p_stats")
        p_logged = sem("p_logged")
        p_rstd = sem("p_rstd")
        p_square = sem("p_square")
        p_scale = sem("p_scale")
        p_normed = sem("p_normed")
        p_turned = sem("p_turned")
        p_turned_sb = sem("p_turned_sb")
        conv_mm = sem("conv_mm")
        conv_sb = sem("conv_sb")
        silu_done = sem("silu_done")
        dbl_mm = sem("dbl_mm")
        dbl_sb = sem("dbl_sb")
        rest1 = sem("rest1")
        part2 = sem("part2")
        rest2 = sem("rest2")
        split_done = sem("split_done")
        dt_mm = sem("dt_mm")
        dt_sb = sem("dt_sb")
        dt_exp = sem("dt_exp")
        dt_log = sem("dt_log")
        delta_done = sem("delta_done")
        du_done = sem("du_done")
        decays = sem("decays")
        bc_done = sem("bc_done")
        fed = sem("fed")
        scanned = sem("scanned")
        read_out = sem("read_out")
        y_sum = sem("y_sum")
        y_skip = sem("y_skip")
        y_gated = sem("y_gated")
        xres_loaded = sem("xres_loaded")
        a_out = sem("a_out")
        a_out_sb = sem("a_out_sb")
        a_h1 = sem("a_h1")
        a_h1_sb = sem("a_h1_sb")
        a_z = sem("a_z")
        a_stats = sem("a_stats")
        a_logged = sem("a_logged")
        a_rstd = sem("a_rstd")
        a_normed = sem("a_normed")
        a_affine = sem("a_affine")
        x1_done = sem("x1_done")
        b_stats = sem("b_stats")
        b_logged = sem("b_logged")
        b_rstd = sem("b_rstd")
        b_normed = sem("b_normed")
        b_turned = sem("b_turned")
        b_turned_sb = sem("b_turned_sb")
        b_xp_mm = sem("b_xp_mm")
        b_xp_sb = sem("b_xp_sb")
        b_gate_mm = sem("b_gate_mm")
        b_gate_sb = sem("b_gate_sb")
        b_fed = sem("b_fed")
        b_scanned = sem("b_scanned")
        b_y_mm = sem("b_y_mm")
        b_y_sb = sem("b_y_sb")
        b_z = sem("b_z")
        b_affine = sem("b_affine")
        x3_done = sem("x3_done")
        stored = sem("stored")

        tmp1 = e1.rows[:, 0, :, :].rearrange("p a b -> p (a b)")
        tmp2 = e1.rows[:, 1, :, :].rearrange("p a b -> p (a b)")
        tmp3 = e1.rows[:, 2, :, :].rearrange("p a b -> p (a b)")
        wq_t = tmp1[0:DK, 0:GR * P].rearrange("c (g d) -> c g d", g=GR)
        key_t = tmp2[0:DK, 0:SIM].rearrange("c (g k) -> c g k", g=GR)
        in_t = tmp2[:, 512:1024]
        wb_t = tmp2[:, 1024:1024 + P]
        taps = tmp3[:, 0:NK * DI].rearrange("p (k d) -> p k d", k=NK)
        rank_i = e1.rows[:, 3, 0:2, :].rearrange("p a b -> p (a b)").bitcast(I32)

        def everywhere(row):
            return row.partition_broadcast(P)

        loads = [
            (in_t, A["in_proj_t"]), (wq_t, A["wq_t"]), (key_t, A["key_t"]), (wb_t, A["wb_t"]),
            (taps.rearrange("p k d -> p (k d)"), everywhere(A["taps"])),
            (ln_w[:], everywhere(A["ln_w"])), (ln_b[:], everywhere(A["ln_b"])),
            (gamma[:], everywhere(A["gamma"])), (beta[:], everywhere(A["beta"])),
            (w_dt[DT0:DT0 + DR, :], A["dt_w_t"]), (w_out[:], A["out_t"]), (w_ff1[:], A["ff1_t"]),
            (w_ff2[:], A["ff2_t"]), (w_xp[:], A["W_in"]), (w_gate[:, IG:IG + NS], A["W_ig"]),
            (w_gate[:, FG:FG + NS], A["W_fg"]), (w_c[FG:FG + NS, :], A["C_mat"]), (w_d[:], A["W_D"]),
            (w_y[:], A["W_out"]), (decay[:], A["A_log"]), (norm_w[:], A["norm_w"]),
            (conv_b[:], A["conv_b"]), (dt_b[:], A["dt_b"]), (d_skip[:], A["Dp"]), (b_ff1[:], A["b1"]),
            (b_ff2[:], A["b2"]), (b_xp[:], A["b_in"]), (b_y[:], A["b_out"]), (b_d[:], A["b_D"]),
            (b_gate[IG:IG + NS, :], A["b_ig"]), (b_gate[FG:FG + NS, :], A["b_fg"]),
            (b_wb[:], A["b_B"]), (b_mat[:], A["B_mat"]),
            (w_xproj[:, :, DT0:DT0 + DR], A["xproj_t"][:, :, 0:DR]),
        ] + [(w_xproj[:, :, r:r + BC], A["xproj_t"][:, :, DR:DR + BC]) for r in PART]

        with nc.Block() as setup:
            @setup.sync
            def _(sp):
                sp.wait_ge(cleared, 1)
                for dst, src in loads:
                    sp.dma_start(dst, src).then_inc(weights_in, 16)

            @setup.gpsimd
            def _(pool):
                pool.memset(ident[:], 0.0).then_inc(made, 1)
                pool.wait_ge(made, 1)
                pool.affine_select(out=ident[:], in_=ident[:], compare_op=ALU.not_equal, fill=1.0, base=0,
                                   pattern=[[-1, P]], channel_multiplier=1).then_inc(made, 1)
                pool.iota(rank_i, pattern=[[0, GR], [-1, KEYS]], base=KEYS, channel_multiplier=0).then_inc(made, 1)

            @setup.vector
            def _(dve):
                for tile in (w_xproj, w_dt, w_gate, w_c, b_gate, hs, gates, dA, xrT, split[0], split[1], dbl):
                    nc.vector.memset(tile[:], 0.0)
                nc.vector.memset(eps[:], EPS).then_inc(cleared, 1)
                dve.wait_ge(made, 3)
                nc.vector.tensor_copy(rank_rev[:], rank_i)
                dve.wait_ge(cleared, 1)
                nc.vector.tensor_tensor(pick[:], ident[:, 0:BC], ident[:, PART[1]:PART[1] + BC],
                                        ALU.add).then_inc(cleared, 1)
                dve.wait_ge(cleared, 2)
                nc.vector.tensor_tensor(pick[:], pick[:], ident[:, PART[2]:PART[2] + BC], ALU.add)
                dve.wait_ge(weights_in, 16 * len(loads))
                nc.vector.tensor_scalar(in_t, in_t, norm_w[:, 0:1], None, ALU.mult).then_inc(cleared, 1)
                dve.wait_ge(cleared, 3)
                nc.vector.tensor_copy(w_res[:], in_t[:, DI:2 * DI])
                for k in range(NK):
                    nc.vector.tensor_tensor(w_taps[:, k, :], in_t[:, 0:DI], taps[:, k, :], ALU.mult)
                nc.vector.tensor_tensor(b_xpy[:], b_xp[:], b_y[:], ALU.add)
                dve.wait_ge(folded, 1)
                nc.vector.tensor_copy(w_sim[:], bank[0][:])
                nc.vector.tensor_copy(w_gate[:, BX:BX + NS], bank[1][:, 0:NS])
                nc.vector.tensor_copy(b_bx[0:NS, :], bank[1][0:NS, NS:NS + 1]).then_inc(cleared, 1)

            @setup.scalar
            def _(act):
                act.wait_ge(weights_in, 16 * len(loads))
                nc.scalar.activation(decay[:], decay[:], ACT.Exp).then_inc(p_scale, 1)
                act.wait_ge(p_scale, 1)
                nc.scalar.mul(decay[:], decay[:], -1.0).then_inc(p_scale, 1)

            @setup.tensor
            def _(pe):
                pe.wait_ge(weights_in, 16 * len(loads))
                for g in range(GR):
                    nc.tensor.matmul(bank[0][:, g * KEYS:(g + 1) * KEYS], wq_t[:, g, :], key_t[:, g, :],
                                     start=True, stop=True, skip_group_check=True)
                nc.tensor.matmul(bank[1][:, 0:NS], wb_t, b_mat[:], start=True, stop=True, skip_group_check=True)
                nc.tensor.matmul(bank[1][0:NS, NS:NS + 1], b_mat[:], b_wb[:], start=True, stop=True,
                                 skip_group_check=True).then_inc(folded, 1)

        P_SCALE0 = 2

        block = ctx.enter_context(nc.Block())

        @block.sync
        def _(sp):
            def iteration(i, q, has):
                b = {p: i + o for p, o in OFFSET.items()}
                if PRE in has:
                    n = b[PRE]
                    if later(n):
                        sp.wait_ge(p_normed, at(n - 1, 1))
                    sp.dma_start(x_in[:], A["x"][n]).then_inc(x_loaded, 16)
                if PA in has:
                    n = b[PA]
                    if later(n):
                        sp.wait_ge(x1_done, at(n - 1, 1))
                    sp.dma_start(x_res[:].rearrange("p (a d) -> p a d", a=NT), A["x"][n]).then_inc(xres_loaded, 16)
                if PC in has:
                    n = b[PC]
                    sp.wait_ge(e2.added, at(n, 1))
                    sp.dma_start(A["y"][n], x3[:]).then_inc(stored, 16)

            run_pipeline(sp, iteration)
            sp.wait_ge(stored, 16 * NB)

        @block.tensor
        def _(pe):
            busy = {}

            def claim(k, i):
                if k in busy:
                    s, per, nth, off = busy[k]
                    pe.wait_ge(s, at(i + off, per, nth))

            def note(k, s, per, nth, off):
                busy[k] = (s, per, nth, off)

            def experts_turn(e, k, i, off):
                n = i + off
                claim(k, i)
                pe.wait_ge(e.normed, at(n, 1))
                for t in range(NT):
                    mm = nc.tensor.transpose(bank[k][:, t * P:(t + 1) * P], e.xn[:, t, :], ident[:])
                mm.then_inc(e.turned, 1)
                note(k, e.turned_sb, 1, 0, off)

            def experts_sim(e, k, i, off, t):
                n = i + off
                claim(k, i)
                if t == 0:
                    pe.wait_ge(e.turned_sb, at(n, 1))
                nc.tensor.matmul(bank[k][:], e.xnT[:, t * P:(t + 1) * P], w_sim[:], start=True,
                                 stop=True).then_inc(e.sim, 1)
                note(k, e.masked, NT, t, off)

            def experts_sum(e, k, i, off):
                n = i + off
                claim(k, i)
                pe.wait_ge(e.scaled, at(n, NT, NT - 1))
                for h in range(HEADS):
                    mm = nc.tensor.matmul(bank[k][:].rearrange("p (t d) -> p t d", t=NT), ident[:],
                                          e.rows[:, :, h, P:2 * P], start=(h == 0), stop=(h == HEADS - 1))
                mm.then_inc(e.summed, 1)
                note(k, e.added, 1, 0, off)

            def iteration(i, q, has):
                for k in busy:
                    s, per, nth, off = busy[k]
                    busy[k] = (s, per, nth, off - 1)
                b = {p: i + o for p, o in OFFSET.items()}

                def broadcast(n):
                    c = b[CORE]
                    if n == 0:
                        pe.wait_ge(split_done, at(c, 1))
                    if n >= 2:
                        pe.wait_ge(read_out, at(c, NS, n - 2))
                    elif later(c):
                        pe.wait_ge(read_out, at(c - 1, NS, NS + n - 2))
                    for w in range(2):
                        r = w * NS + n
                        mm = nc.tensor.matmul(bcast[n % 2][:, w, :], pick[:, r:r + 1].to_broadcast([P, P]),
                                              split[q][:], start=True, stop=True)
                    mm.then_inc(bc_done, 1)

                for n in range(NS):
                    if CORE in has:
                        if n == 0:
                            broadcast(0)
                        if n + 1 < NS:
                            broadcast(n + 1)
                        c = b[CORE]
                        if n == 0 and later(c):
                            pe.wait_ge(y_skip, at(c - 1, 1))
                        pe.wait_ge(read_out, at(c, NS, n))
                        for j in range(NH):
                            mm = nc.tensor.matmul(ysum[:, j, :], ident[:], hp[:, n % NP, j, :],
                                                  start=(n == 0), stop=(n == NS - 1))
                        mm.then_inc(y_sum, 1)
                    if PA in has:
                        a = b[PA]
                        if n == 0:
                            claim(0, i)
                            pe.wait_ge(y_gated, at(a, 1))
                            for j in range(NH):
                                nc.tensor.matmul(bank[0][:], w_out[:, j, :], ucs[1 - q][:, j, :], start=(j == 0),
                                                 stop=False, skip_group_check=True)
                            for t in range(NT):
                                mm = nc.tensor.matmul(bank[0][:, t * P:(t + 1) * P], xn0[1 - q][:, t, :], ident[:],
                                                      start=False, stop=True, skip_group_check=True)
                            mm.then_inc(a_out, 1)
                            note(0, a_out_sb, 1, 0, OFFSET[PA])
                        if n == 1:
                            claim(0, i)
                            pe.wait_ge(a_out_sb, at(a, 1))
                            nc.tensor.matmul(bank[0][:], w_ff1[:], outT[:], start=True, stop=True).then_inc(a_h1, 1)
                            note(0, a_h1_sb, 1, 0, OFFSET[PA])
                        if n == 2:
                            claim(0, i)
                            pe.wait_ge(a_h1_sb, at(a, 1))
                            for t in range(NT):
                                tok = slice(t * P, (t + 1) * P)
                                nc.tensor.matmul(bank[0][:, tok], h1T[:, tok], w_ff2[:], start=True, stop=False,
                                                 skip_group_check=True)
                                mm = nc.tensor.matmul(bank[0][:, tok], outTb[:, tok], ident[:], start=False,
                                                      stop=True, skip_group_check=True)
                            mm.then_inc(a_z, 1)
                            note(0, a_normed, 1, 0, OFFSET[PA])
                        if n == 7:
                            experts_turn(e1, 0, i, OFFSET[PA])
                        if 8 <= n < 8 + NT:
                            experts_sim(e1, 0, i, OFFSET[PA], n - 8)
                    if PRE in has:
                        p = b[PRE]
                        if n == 3:
                            claim(0, i)
                            pe.wait_ge(p_normed, at(p, 1))
                            for t in range(NT):
                                mm = nc.tensor.transpose(bank[0][:, t * P:(t + 1) * P], xr[:, t, :], ident[:])
                            mm.then_inc(p_turned, 1)
                            note(0, p_turned_sb, 1, 0, OFFSET[PRE])
                        if 4 <= n < 6:
                            j = n - 4
                            claim(0, i)
                            if j == 0:
                                pe.wait_ge(p_turned_sb, at(p, 1))
                            for k in range(NK):
                                mm = nc.tensor.matmul(bank[0][:], w_taps[:, k, j * P:(j + 1) * P], xrT[:, k:k + T],
                                                      start=(k == 0), stop=(k == NK - 1))
                            mm.then_inc(conv_mm, 1)
                            note(0, conv_sb, 2 * NH, j, OFFSET[PRE])
                        if n == 6:
                            for j in range(NH):
                                claim(0, i)
                                nc.tensor.matmul(bank[0][:], w_res[:, j * P:(j + 1) * P], xrT[:, NK - 1:NK - 1 + T],
                                                 start=True, stop=True).then_inc(conv_mm, 1)
                                note(0, conv_sb, 2 * NH, NH + j, OFFSET[PRE])
                        if n == 12:
                            claim(0, i)
                            pe.wait_ge(silu_done, at(p, 1))
                            for j in range(NH):
                                mm = nc.tensor.matmul(bank[0][:], w_xproj[:, j, :], ucs[1 - q][:, j, :],
                                                      start=(j == 0), stop=(j == NH - 1))
                            mm.then_inc(dbl_mm, 1)
                            note(0, dbl_sb, 1, 0, OFFSET[PRE])
                        if n == 13:
                            for j in range(NH):
                                claim(0, i)
                                if j == 0:
                                    pe.wait_ge(dbl_sb, at(p, 1))
                                nc.tensor.matmul(bank[0][:], w_dt[:, j * P:(j + 1) * P], dbl[:], start=True,
                                                 stop=True).then_inc(dt_mm, 1)
                                note(0, dt_sb, NH, j, OFFSET[PRE])
                    if PB in has:
                        m = b[PB]
                        if n == 3:
                            experts_sum(e1, 1, i, OFFSET[PB])
                        if n == 5:
                            claim(1, i)
                            pe.wait_ge(b_normed, at(m, 2, 0))
                            for t in range(NT):
                                mm = nc.tensor.transpose(bank[1][:, t * P:(t + 1) * P], xnb[:, t, :], ident[:])
                            mm.then_inc(b_turned, 1)
                            note(1, b_turned_sb, 1, 0, OFFSET[PB])
                        if n == 6:
                            claim(1, i)
                            pe.wait_ge(b_turned_sb, at(m, 1))
                            nc.tensor.matmul(bank[1][:], w_xp[:], xnbT[:], start=True, stop=True).then_inc(b_xp_mm, 1)
                            note(1, b_xp_sb, 1, 0, OFFSET[PB])
                            claim(1, i)
                            nc.tensor.matmul(bank[1][:], w_gate[:], xpT[:], start=True, stop=True).then_inc(b_gate_mm, 1)
                            note(1, b_fed, 1, 0, OFFSET[PB])
                        if n == 7:
                            claim(1, i)
                            nc.tensor.matmul(bank[1][:], w_d[:], xpT[:], start=True, stop=False)
                            pe.wait_ge(b_scanned, at(m, 1))
                            nc.tensor.matmul(bank[1][:], w_c[:], hs[:], start=False, stop=True).then_inc(b_y_mm, 1)
                            note(1, b_y_sb, 1, 0, OFFSET[PB])
                        if n == 8:
                            claim(1, i)
                            pe.wait_ge(b_y_sb, at(m, 1))
                            for t in range(NT):
                                tok = slice(t * P, (t + 1) * P)
                                nc.tensor.matmul(bank[1][:, tok], xnbT[:, tok], w_y[:], start=True, stop=False,
                                                 skip_group_check=True)
                                mm = nc.tensor.matmul(bank[1][:, tok], xpTb[:, tok], ident[:], start=False,
                                                      stop=True, skip_group_check=True)
                            mm.then_inc(b_z, 1)
                            note(1, b_normed, 2, 1, OFFSET[PB])
                        if n == 11:
                            experts_turn(e2, 1, i, OFFSET[PB])
                        if 12 <= n < 12 + NT:
                            experts_sim(e2, 1, i, OFFSET[PB], n - 12)
                    if PC in has:
                        if n == 9:
                            experts_sum(e2, 1, i, OFFSET[PC])

            run_pipeline(pe, iteration)

        @block.scalar
        def _(act):
            def rstd(mv, ln, rs, stats, per, nth, logged, ln_at, done):
                act.wait_ge(*stats)
                nc.scalar.activation(ln[:], mv[:, :, 1], ACT.Ln, bias=eps[:, 0:1]).then_inc(logged, 1)
                act.wait_ge(logged, ln_at)
                nc.scalar.activation(rs[:], ln[:], ACT.Exp, scale=-0.5).then_inc(done, 1)

            def experts_rstd(e, n):
                act.wait_ge(e.stats, at(n, 2, 1))
                nc.scalar.activation(e.ln[:], e.mv[:, :, 1], ACT.Ln, bias=eps[:, 0:1]).then_inc(e.logged, 1)
                act.wait_ge(e.logged, at(n, 1))
                nc.scalar.activation(e.rs[:], e.ln[:], ACT.Exp, scale=-0.5).then_inc(e.rstd, 1)

            def experts_turned(e, k, n):
                act.wait_ge(e.turned, at(n, 1))
                nc.scalar.activation(e.xnT[:], bank[k][:], ACT.Copy).then_inc(e.turned_sb, 1)

            def experts_gelu(e, n):
                act.wait_ge(e.dotted, at(n, NT, NT - 1))
                nc.scalar.activation(e.act[:], e.dot[:], ACT.Gelu).then_inc(e.gelu, 1)

            def experts_scale(e, n, t):
                if t == 0:
                    act.wait_ge(e.weighed, at(n, 1))
                for h in range(HEADS):
                    row = e.rows[:, t, h, P:2 * P]
                    op = nc.scalar.activation(row, row, ACT.Copy, scale=e.coef[:, t, h:h + 1])
                op.then_inc(e.scaled, 1)

            def iteration(i, q, has):
                b = {p: i + o for p, o in OFFSET.items()}

                def decays_of(n):
                    c = b[CORE]
                    if n == 0:
                        act.wait_ge(delta_done, at(c, 1))
                    if n >= NDA:
                        act.wait_ge(scanned, at(c, NS, n - NDA))
                    elif later(c):
                        act.wait_ge(scanned, at(c - 1, NS, NS + n - NDA))
                    for j in range(NH):
                        op = nc.scalar.activation(dA[:, n % NDA, j, 1:T], delta[q][:, j, 1:T], ACT.Exp,
                                                  scale=decay[:, j, n:n + 1])
                    op.then_inc(decays, 1)

                for n in range(NS):
                    if CORE in has:
                        for m in range(LEAD + 1) if n == 0 else [n + LEAD] if n + LEAD < NS else []:
                            decays_of(m)
                    if PA in has:
                        a = b[PA]
                        if n == 1:
                            act.wait_ge(a_out, at(a, 1))
                            if later(a):
                                act.wait_ge(x1_done, at(a - 1, 1))
                            nc.scalar.activation(outT[:], bank[0][:], ACT.Copy)
                            nc.scalar.activation(outTb[:], bank[0][:], ACT.Identity,
                                                 bias=b_ff2[:, 0:1]).then_inc(a_out_sb, 1)
                        if n == 2:
                            act.wait_ge(a_h1, at(a, 1))
                            nc.scalar.activation(h1T[:], bank[0][:], ACT.Gelu, bias=b_ff1[:, 0:1]).then_inc(a_h1_sb, 1)
                        if n == 3:
                            act.wait_ge(a_stats, at(a, 2, 1))
                            nc.scalar.activation(lnA[:], mvA[:, :, 1], ACT.Ln, bias=eps[:, 0:1]).then_inc(a_logged, 1)
                            act.wait_ge(a_logged, at(a, 1))
                            nc.scalar.activation(rsA[:], lnA[:], ACT.Exp, scale=-0.5).then_inc(a_rstd, 1)
                        if n == 6:
                            experts_rstd(e1, a)
                        if n == 7:
                            experts_turned(e1, 0, a)
                    if PRE in has:
                        p = b[PRE]
                        if n == 1:
                            act.wait_ge(p_stats, at(p, 2, 1))
                            nc.scalar.activation(ln0[:], mv0[:, :, 1], ACT.Ln, bias=eps[:, 0:1]).then_inc(p_logged, 1)
                            act.wait_ge(p_logged, at(p, 2, 0))
                            nc.scalar.activation(rs0[:], ln0[:], ACT.Exp, scale=-0.5).then_inc(p_rstd, 1)
                        if n == 2:
                            act.wait_ge(p_square, at(p, 2, 1))
                            nc.scalar.activation(ln0[:], m20[:], ACT.Ln, bias=eps[:, 0:1]).then_inc(p_logged, 1)
                            act.wait_ge(p_logged, at(p, 2, 1))
                            nc.scalar.activation(rr0[:], ln0[:], ACT.Exp, scale=-0.5).then_inc(p_rstd, 1)
                        if n == 4:
                            act.wait_ge(p_turned, at(p, 1))
                            nc.scalar.activation(xrT[:, NK - 1:NK - 1 + T], bank[0][:], ACT.Copy)\
                                .then_inc(p_turned_sb, 1)
                        for j in {5: [0], 6: [1, 2, 3]}.get(n, []):
                            act.wait_ge(conv_mm, at(p, 2 * NH, j))
                            if j == 0 and second(p):
                                act.wait_ge(a_out, at(p - 2, 1))
                            if j < NH:
                                op = nc.scalar.activation(ucs[1 - q][:, j, :], bank[0][:], ACT.Identity,
                                                          bias=conv_b[:, j:j + 1])
                            else:
                                op = nc.scalar.activation(ucs[1 - q][:, j, :], bank[0][:], ACT.Copy)
                            op.then_inc(conv_sb, 1)
                        if n == 10:
                            act.wait_ge(conv_sb, at(p, 2 * NH, 2 * NH - 1))
                            nc.scalar.activation(ucs[1 - q][:], ucs[1 - q][:], ACT.Silu).then_inc(silu_done, 1)
                        if n == 12:
                            act.wait_ge(dbl_mm, at(p, 1))
                            nc.scalar.activation(dbl[:], bank[0][:], ACT.Copy)
                            nc.scalar.activation(split[1 - q][:], bank[0][:], ACT.Copy)\
                                .then_inc(dbl_sb, 1)
                        if n == 13:
                            act.wait_ge(rest1, at(p, 1))
                            nc.scalar.activation(split[1 - q][PART[1]:, :], rest[PART[1]:, :], ACT.Copy)\
                                .then_inc(part2, 1)
                            if later(p):
                                act.wait_ge(delta_done, at(p - 1, 1))
                            for j in range(NH):
                                act.wait_ge(dt_mm, at(p, NH, j))
                                nc.scalar.activation(soft[:, j, :], bank[0][:], ACT.Abs, bias=dt_b[:, j:j + 1])
                                nc.scalar.activation(delta[1 - q][:, j, :], bank[0][:], ACT.Relu,
                                                     bias=dt_b[:, j:j + 1]).then_inc(dt_sb, 1)
                            act.wait_ge(rest2, at(p, 1))
                            nc.scalar.activation(split[1 - q][PART[2]:, :], rest[PART[2]:, :], ACT.Copy)\
                                .then_inc(split_done, 1)
                        if n == 14:
                            act.wait_ge(dt_sb, at(p, NH, NH - 1))
                            nc.scalar.activation(soft[:], soft[:], ACT.Exp, scale=-1.0).then_inc(dt_exp, 1)
                            act.wait_ge(dt_exp, at(p, 1))
                            nc.scalar.activation(soft[:], soft[:], ACT.Ln, bias=1.0).then_inc(dt_log, 1)
                    if PB in has:
                        m = b[PB]
                        if n == 2:
                            experts_gelu(e1, m)
                        if n in (2, 3):
                            for t in range(2 * (n - 2), 2 * (n - 2) + 2):
                                experts_scale(e1, m, t)
                        if n == 4:
                            act.wait_ge(b_stats, at(m, 4, 1))
                            nc.scalar.activation(lnB[:], mvB[:, :, 1], ACT.Ln, bias=eps[:, 0:1]).then_inc(b_logged, 1)
                            act.wait_ge(b_logged, at(m, 2, 0))
                            nc.scalar.activation(rsB[:], lnB[:], ACT.Exp, scale=-0.5).then_inc(b_rstd, 1)
                        if n == 6:
                            act.wait_ge(b_turned, at(m, 1))
                            nc.scalar.activation(xnbT[:], bank[1][:], ACT.Copy).then_inc(b_turned_sb, 1)
                            act.wait_ge(b_xp_mm, at(m, 1))
                            nc.scalar.activation(xpT[:], bank[1][:], ACT.Identity, bias=b_xp[:, 0:1])
                            nc.scalar.activation(xpTb[:], bank[1][:], ACT.Identity,
                                                 bias=b_xpy[:, 0:1]).then_inc(b_xp_sb, 1)
                        if n == 7:
                            act.wait_ge(b_gate_mm, at(m, 1))
                            nc.scalar.activation(gates[0:FG + NS, :], bank[1][0:FG + NS, :], ACT.Sigmoid,
                                                 bias=b_gate[0:FG + NS, 0:1]).then_inc(b_gate_sb, 1)
                        if n == 8:
                            act.wait_ge(b_y_mm, at(m, 1))
                            nc.scalar.activation(xnbT[:], bank[1][:], ACT.Tanh, bias=b_d[:, 0:1]).then_inc(b_y_sb, 1)
                        if n == 9:
                            act.wait_ge(b_stats, at(m, 4, 3))
                            nc.scalar.activation(lnB[:], mvB[:, :, 1], ACT.Ln, bias=eps[:, 0:1]).then_inc(b_logged, 1)
                            act.wait_ge(b_logged, at(m, 2, 1))
                            nc.scalar.activation(rsB[:], lnB[:], ACT.Exp, scale=-0.5).then_inc(b_rstd, 1)
                        if n == 11:
                            experts_rstd(e2, m)
                        if n == 12:
                            experts_turned(e2, 1, m)
                    if PC in has:
                        if n == 8:
                            experts_gelu(e2, b[PC])
                        if n in (8, 9):
                            for t in range(2 * (n - 8), 2 * (n - 8) + 2):
                                experts_scale(e2, b[PC], t)

            run_pipeline(act, iteration)

        @block.vector
        def _(dve):
            def statistics(src, st, mv, s, base):
                for t in range(NT):
                    op = nc.vector.bn_stats(st[:, t, :], src[:, t, :])
                op.then_inc(s, 1)
                dve.wait_ge(s, base)
                nc.vector.memset(idle_dve[:], 0.0)
                for t in range(NT):
                    op = nc.vector.bn_aggr(mv[:, t, :], st[:, t, :])
                op.then_inc(s, 1)

            def normalise(dst, src, mv, scale, s):
                for t in range(NT):
                    op = nc.vector.tensor_scalar(dst[:, t, :], src[:, t, :], mv[:, t, 0:1], scale[:, t:t + 1],
                                                 ALU.subtract, ALU.mult)
                if s is not None:
                    op.then_inc(s, 1)

            def experts_xn(e, n, x):
                dve.wait_ge(e.rstd, at(n, 1))
                normalise(e.xn, x, e.mv, e.rs, e.normed)

            def experts_top(e, k, n, t):
                dve.wait_ge(e.sim, at(n, NT, t))
                sims = bank[k][:].rearrange("p (g k) -> p g k", g=GR)
                nc.vector.tensor_reduce(e.top[:, t, :], sims, AX_X, ALU.max).then_inc(e.topped, 1)
                dve.wait_ge(e.topped, at(n, NT, t))
                nc.vector.tensor_tensor(e.mask[:, t, :].rearrange("p (g k) -> p g k", g=GR), sims,
                                        e.top[:, t, :].unsqueeze(2).to_broadcast([P, GR, KEYS]),
                                        ALU.is_equal).then_inc(e.masked, 1)

            def experts_index(e, n):
                dve.wait_ge(e.masked, at(n, NT, NT - 1))
                nc.vector.tensor_tensor(e.mask[:], e.mask[:], rank_rev[:].unsqueeze(1).to_broadcast([P, NT, SIM]),
                                        ALU.mult).then_inc(e.picks, 1)
                dve.wait_ge(e.picks, at(n, 3, 0))
                nc.vector.tensor_reduce(e.rank[:], e.mask[:].rearrange("p t (g k) -> p t g k", g=GR), AX_X,
                                        ALU.max).then_inc(e.picks, 1)
                dve.wait_ge(e.picks, at(n, 3, 1))
                nc.vector.scalar_tensor_tensor(out=e.code[:], in0=e.rank[:, :, 0:HEADS], scalar=-float(KEYS),
                                               in1=e.rank[:, :, HEADS:GR], op0=ALU.mult,
                                               op1=ALU.subtract).then_inc(e.picks, 1)
                dve.wait_ge(e.picks, at(n, 3, 2))
                nc.vector.tensor_tensor(e.score[:], e.top[:, :, 0:HEADS], e.top[:, :, HEADS:GR], ALU.add)
                nc.vector.tensor_scalar(e.index[:], e.code[:], float(KEYS * KEYS + KEYS), None,
                                        ALU.add).then_inc(e.indexed, 1)

            def experts_dot(e, n, t):
                dve.wait_ge(e.fetched[t], (n + 1) * (16 * HEADS))
                for h in range(HEADS):
                    row = e.rows[:, t, h, 0:P]
                    op = nc.vector.tensor_tensor_reduce(row, row, e.xn[:, t, :], 1.0, 0.0, ALU.mult, ALU.add,
                                                        e.dot[:, t, h:h + 1])
                op.then_inc(e.dotted, 1)

            def experts_weigh(e, n):
                dve.wait_ge(e.gelu, at(n, 1))
                nc.vector.scalar_tensor_tensor(out=e.coef[:], in0=e.score[:], scalar=0.0, in1=e.act[:], op0=ALU.max,
                                               op1=ALU.mult).then_inc(e.weighed, 1)

            def iteration(i, q, has):
                b = {p: i + o for p, o in OFFSET.items()}
                for n in range(NS):
                    if CORE in has:
                        c = b[CORE]
                        state = hp[:, n % NP, :, :]
                        flat = state.rearrange("p a b -> p (a b)")
                        if n == 0:
                            dve.wait_ge(du_done, at(c, 1))
                        dve.wait_ge(bc_done, at(c, NS, n))
                        if n >= NP:
                            dve.wait_ge(y_sum, at(c, NS, n - NP))
                        elif later(c):
                            dve.wait_ge(y_sum, at(c - 1, NS, NS + n - NP))
                        nc.vector.tensor_tensor(state, du[q][:],
                                                bcast[n % 2][:, 0:1, :].to_broadcast([P, NH, T]),
                                                ALU.mult).then_inc(fed, 1)
                        dve.wait_ge(decays, at(c, NS, n))
                        dve.wait_ge(fed, at(c, NS, n))
                        nc.vector.tensor_tensor_scan(flat, dA[:, n % NDA, :, :].rearrange("p a b -> p (a b)"), flat,
                                                     0.0, ALU.mult, ALU.add).then_inc(scanned, 1)
                        dve.wait_ge(scanned, at(c, NS, n))
                        nc.vector.tensor_tensor(state, state,
                                                bcast[n % 2][:, 1:2, :].to_broadcast([P, NH, T]),
                                                ALU.mult).then_inc(read_out, 1)
                    if PA in has:
                        a = b[PA]
                        if n == 3:
                            dve.wait_ge(a_z, at(a, 1))
                            statistics(bank[0][:].rearrange("p (t d) -> p t d", t=NT), stA, mvA, a_stats, at(a, 2, 0))
                        if n == 4:
                            dve.wait_ge(a_rstd, at(a, 1))
                            normalise(outT[:].rearrange("p (t d) -> p t d", t=NT),
                                      bank[0][:].rearrange("p (t d) -> p t d", t=NT), mvA, rsA, a_normed)
                        if n == 6:
                            dve.wait_ge(x1_done, at(a, 1))
                            statistics(x1, e1.st, e1.mv, e1.stats, at(a, 2, 0))
                        if n == 7:
                            experts_xn(e1, a, x1)
                        if 9 <= n < 9 + NT:
                            experts_top(e1, 0, a, n - 9)
                        if n == 12:
                            experts_index(e1, a)
                    if PRE in has:
                        p = b[PRE]
                        if n == 1:
                            dve.wait_ge(x_loaded, (p + 1) * 16)
                            statistics(x_in, st0, mv0, p_stats, at(p, 2, 0))
                        if n == 2:
                            dve.wait_ge(p_rstd, at(p, 2, 0))
                            nc.vector.tensor_tensor(m20[:], mv0[:, :, 1], rs0[:], ALU.mult).then_inc(p_square, 1)
                            dve.wait_ge(p_square, at(p, 2, 0))
                            nc.vector.tensor_tensor(m20[:], m20[:], rs0[:], ALU.mult).then_inc(p_square, 1)
                        if n == 3:
                            dve.wait_ge(p_rstd, at(p, 2, 1))
                            nc.vector.tensor_tensor(s20[:], rs0[:], rr0[:], ALU.mult).then_inc(p_scale, 1)
                            if second(p):
                                dve.wait_ge(a_out, at(p - 2, 1))
                            normalise(xn0[1 - q], x_in, mv0, rs0, None)
                            dve.wait_ge(p_scale, P_SCALE0 + at(p, 1))
                            if later(p):
                                dve.wait_ge(p_turned, at(p - 1, 1))
                            normalise(xr, x_in, mv0, s20, p_normed)
                    if PB in has:
                        m = b[PB]
                        if n == 0:
                            experts_dot(e1, m, 0)
                            experts_dot(e1, m, 1)
                        if n == 1:
                            experts_dot(e1, m, 2)
                            experts_dot(e1, m, 3)
                        if n == 2:
                            experts_weigh(e1, m)
                        if n == 4:
                            dve.wait_ge(e1.summed, at(m, 1))
                            nc.vector.tensor_tensor(x2[:], bank[1][:].rearrange("p (t d) -> p t d", t=NT), x1[:],
                                                    ALU.add).then_inc(e1.added, 1)
                            dve.wait_ge(e1.added, at(m, 1))
                            statistics(x2, stB, mvB, b_stats, at(m, 4, 0))
                        if n == 5:
                            dve.wait_ge(b_rstd, at(m, 2, 0))
                            if later(m):
                                dve.wait_ge(x3_done, at(m - 1, 1))
                            normalise(xnb, x2, mvB, rsB, b_normed)
                        if n == 7:
                            dve.wait_ge(b_gate_sb, at(m, 1))
                            nc.vector.scalar_tensor_tensor(out=hs[FG:FG + NS, :], in0=bank[1][BX:BX + NS, :],
                                                           scalar=b_bx[0:NS, 0:1], in1=gates[IG:IG + NS, :],
                                                           op0=ALU.add, op1=ALU.mult).then_inc(b_fed, 1)
                            dve.wait_ge(b_fed, at(m, 1))
                            nc.vector.tensor_tensor_scan(hs[FG:FG + NS, :], gates[FG:FG + NS, :], hs[FG:FG + NS, :],
                                                         0.0, ALU.mult, ALU.add).then_inc(b_scanned, 1)
                        if n == 9:
                            dve.wait_ge(b_z, at(m, 1))
                            statistics(bank[1][:].rearrange("p (t d) -> p t d", t=NT), stB, mvB, b_stats,
                                       at(m, 4, 2))
                            dve.wait_ge(b_rstd, at(m, 2, 1))
                            normalise(xnb, bank[1][:].rearrange("p (t d) -> p t d", t=NT), mvB, rsB, b_normed)
                        if n == 11:
                            dve.wait_ge(x3_done, at(m, 1))
                            statistics(x3, e2.st, e2.mv, e2.stats, at(m, 2, 0))
                            experts_xn(e2, m, x3)
                        if 13 <= n:
                            experts_top(e2, 1, m, n - 13)
                        if n == NS - 1:
                            experts_top(e2, 1, m, 3)
                            experts_index(e2, m)
                    if PC in has:
                        g = b[PC]
                        if 4 <= n < 4 + NT:
                            experts_dot(e2, g, n - 4)
                        if n == 8:
                            experts_weigh(e2, g)
                        if n == 10:
                            dve.wait_ge(e2.summed, at(g, 1))
                            nc.vector.tensor_tensor(x3[:], bank[1][:].rearrange("p (t d) -> p t d", t=NT), x3[:],
                                                    ALU.add).then_inc(e2.added, 1)
                if CORE in has:
                    c = b[CORE]
                    dve.wait_ge(y_sum, at(c, NS, NS - 1))
                    for j in range(NH):
                        op = nc.vector.scalar_tensor_tensor(out=ucs[q][:, j, :], in0=ucs[q][:, j, :],
                                                            scalar=d_skip[:, j:j + 1], in1=ysum[:, j, :],
                                                            op0=ALU.mult, op1=ALU.add)
                    op.then_inc(y_skip, 1)
                    dve.wait_ge(y_skip, at(c, 1))
                    nc.vector.tensor_tensor(ucs[q][:, 0:NH, :], ucs[q][:, 0:NH, :], ucs[q][:, NH:2 * NH, :],
                                            ALU.mult).then_inc(y_gated, 1)

            run_pipeline(dve, iteration)

        @block.gpsimd
        def _(pool):
            def fetch(e, n, t):
                if t == 0:
                    pool.wait_ge(e.indexed, at(n, 1))
                    if later(n):
                        pool.wait_ge(e.summed, at(n - 1, 1))
                        pool.wait_ge(e.started, at(n - 1, 1))
                    pool.tensor_tensor(e.mark[:], eps[:], eps[:], ALU.add).then_inc(e.started, 1)
                for h in range(HEADS):
                    pool.indirect_dma_start(
                        e.rows[:, t, h, :], None, A["experts"],
                        bass.IndirectOffsetOnAxis(ap=e.index[:, t, h:h + 1], axis=0)).then_inc(e.fetched[t], 16)

            def iteration(i, q, has):
                b = {p: i + o for p, o in OFFSET.items()}
                for n in range(NS):
                    if PC in has and n < NT:
                        fetch(e2, b[PC], n)
                    if PA in has and n == 5:
                        a = b[PA]
                        z = outT[:].rearrange("p (t d) -> p t d", t=NT)
                        pool.wait_ge(a_normed, at(a, 1))
                        pool.wait_ge(xres_loaded, (a + 1) * 16)
                        if later(a):
                            pool.wait_ge(e1.added, at(a - 1, 1))
                        pool.tensor_tensor(z, z, ln_w[:].unsqueeze(1).to_broadcast([P, NT, P]),
                                           ALU.mult).then_inc(a_affine, 1)
                        pool.wait_ge(a_affine, at(a, 2, 0))
                        pool.tensor_tensor(z, z, ln_b[:].unsqueeze(1).to_broadcast([P, NT, P]),
                                           ALU.add).then_inc(a_affine, 1)
                        pool.wait_ge(a_affine, at(a, 2, 1))
                        pool.tensor_tensor(x1[:], z, x_res[:].rearrange("p (t d) -> p t d", t=NT),
                                           ALU.add).then_inc(x1_done, 1)
                    if PB in has and n == 10:
                        m = b[PB]
                        pool.wait_ge(b_normed, at(m, 2, 1))
                        pool.tensor_tensor(xnb[:], xnb[:], gamma[:].unsqueeze(1).to_broadcast([P, NT, P]),
                                           ALU.mult).then_inc(b_affine, 1)
                        pool.wait_ge(b_affine, at(m, 2, 0))
                        pool.tensor_tensor(xnb[:], xnb[:], beta[:].unsqueeze(1).to_broadcast([P, NT, P]),
                                           ALU.add).then_inc(b_affine, 1)
                        pool.wait_ge(b_affine, at(m, 2, 1))
                        if later(m):
                            pool.wait_ge(stored, m * 16)
                        pool.tensor_tensor(x3[:], xnb[:], x2[:], ALU.add).then_inc(x3_done, 1)
                    if PA in has and n == 12:
                        fetch(e1, b[PA], 0)
                    if PRE in has and n == 13:
                        p = b[PRE]
                        pool.wait_ge(dbl_sb, at(p, 1))
                        pool.tensor_tensor(rest[:], dbl[:], split[1 - q][:], ALU.subtract).then_inc(rest1, 1)
                        pool.wait_ge(part2, at(p, 1))
                        pool.tensor_tensor(rest[:], rest[:], split[1 - q][:], ALU.subtract).then_inc(rest2, 1)
                    if PA in has and n == 13:
                        fetch(e1, b[PA], 1)
                    if PRE in has and n == 14:
                        p = b[PRE]
                        pool.wait_ge(dt_log, at(p, 1))
                        pool.tensor_tensor(delta[1 - q][:], delta[1 - q][:], soft[:], ALU.add).then_inc(delta_done, 1)
                        pool.wait_ge(delta_done, at(p, 1))
                        if second(p):
                            pool.wait_ge(fed, at(p - 2, NS, NS - 1))
                        pool.tensor_tensor(du[1 - q][:], delta[1 - q][:], ucs[1 - q][:, 0:NH, :],
                                           ALU.mult).then_inc(du_done, 1)
                    if PA in has and n == 14:
                        fetch(e1, b[PA], 2)
                        fetch(e1, b[PA], 3)

            run_pipeline(pool, iteration)


def kernel(**inputs):
    import numpy as np
    import concourse.bacc as bacc
    from concourse.bass_utils import run_bass_kernel_spmd

    def a(name):
        return np.asarray(inputs["L0_attn_a_" + name])

    def b(name):
        return np.asarray(inputs["L0_attn_b_" + name])

    def f(name):
        return np.asarray(inputs["L0_ffn_" + name])

    def halves(v):
        return v.reshape(NH, P, -1).transpose(1, 0, 2)

    data = {
        "x": a("x"),
        "in_proj_t": a("in_proj_w").T,
        "taps": a("conv_w").T.reshape(NK * DI),
        "norm_w": a("norm_w")[:, None],
        "conv_b": halves(a("conv_b"))[:, :, 0],
        "xproj_t": halves(a("x_proj_w").T),
        "dt_w_t": a("dt_w").T,
        "dt_b": halves(a("dt_b"))[:, :, 0],
        "A_log": halves(a("A_log")),
        "Dp": halves(a("Dp"))[:, :, 0],
        "out_t": halves(a("out_proj_w").T),
        "ff1_t": a("ff_w1").T, "b1": a("ff_b1")[:, None],
        "ff2_t": a("ff_w2").T, "b2": a("ff_b2")[:, None],
        "ln_w": a("ff_ln_w"), "ln_b": a("ff_ln_b"),
        "W_in": b("W_in"), "b_in": b("b_in")[:, None],
        "wb_t": b("W_B").T, "b_B": b("b_B")[:, None], "B_mat": b("B_mat"), "C_mat": b("C_mat"),
        "W_D": b("W_D"), "b_D": b("b_D")[:, None], "W_out": b("W_out"), "b_out": b("b_out")[:, None],
        "W_ig": b("W_ig"), "b_ig": b("b_ig")[:, None], "W_fg": b("W_fg"), "b_fg": b("b_fg")[:, None],
        "gamma": b("gamma"), "beta": b("beta"),
        "wq_t": f("w_q").T.reshape(GR, DK, P).transpose(1, 0, 2),
        "key_t": f("keys").transpose(3, 2, 0, 1).reshape(DK, GR, KEYS),
        "experts": np.concatenate([f("w_down"), f("w_up")], axis=1),
    }
    data = {k: np.ascontiguousarray(v) for k, v in data.items()}

    nc = bacc.Bacc("TRN2", target_bir_lowering=False, num_devices=1)
    tensors = {k: nc.dram_tensor("in_" + k, v.shape, mybir.dt.from_np(v.dtype), kind="ExternalInput").ap()
               for k, v in data.items()}
    tensors["x"] = tensors["x"].rearrange("b (t p) d -> b p t d", p=P)
    y = nc.dram_tensor("y", (NB, T, P), F32, kind="ExternalOutput").ap()
    tensors["y"] = y.rearrange("b (t p) d -> b p t d", p=P)
    build(nc, tensors)
    return run_bass_kernel_spmd(nc, [{"in_" + k: v for k, v in data.items()}], core_ids=[0]).results[0]["y"]
```

```python
from contextlib import ExitStack

import concourse.bass as bass
from concourse import mybir

ALU = mybir.AluOpType
ACT = mybir.ActivationFunctionType
F32 = mybir.dt.float32
BF16 = mybir.dt.bfloat16
I32 = mybir.dt.int32
U32 = mybir.dt.uint32
AX_X = mybir.AxisListType.X

P = 128
NB, T = 16, 512
NT = T // P
DI = 256
NH = DI // P
NS = 16
NK = 4
DR = 8
HEADS, KEYS, DK = 8, 32, 64
GR = 2 * HEADS
SIM = GR * KEYS
EPS = 1e-5
EXP_AND_LN = "natural_log_exp_and_others"

BC = 2 * NS
PART = (0, 64, 96)
DT0 = 32
IG, FG, BX = 0, 32, 64

NDA = 4
NBC = 3
NP = 2
LEAD = 3

PRE, CORE, PA, PB, PC, PD = "pre", "core", "A", "B", "C", "D"
OFFSET = {PRE: 1, CORE: 0, PA: -1, PB: -2, PC: -3, PD: -4}
LAST_ITERATION = NB - 1 + 4
LOOP_FROM, LOOP_TO = 5, 15


def at(b, per, k=0):
    return b * per + (k + 1)


def later(b):
    return not (isinstance(b, int) and b == 0)


def second(b):
    return not (isinstance(b, int) and b < 2)


def phases(i):
    return {p for p, o in OFFSET.items() if 0 <= i + o < NB}


def run_pipeline(eng, iteration):
    iteration(-1, 1, phases(-1))
    for i in range(LOOP_FROM):
        iteration(i, i % 2, phases(i))
    every = set(OFFSET)
    with eng.Fori(LOOP_FROM, LOOP_TO - 1, 2) as i:
        iteration(i, LOOP_FROM % 2, every)
        iteration(i + 1, 1 - LOOP_FROM % 2, every)
    for i in range(LOOP_TO, LAST_ITERATION + 1):
        iteration(i, i % 2, phases(i))


def build(nc, A):
    with ExitStack() as ctx:
        def sb(name, shape, dt=F32):
            return ctx.enter_context(nc.sbuf_tensor(name, shape, dt))

        def sem(name):
            return ctx.enter_context(nc.semaphore(name))

        ident = sb("ident", [P, P])
        pick = sb("pick", [P, BC], BF16)
        w_taps = sb("w_taps", [P, NK, DI])
        w_res = sb("w_res", [P, DI])
        w_xproj = sb("w_xproj", [P, NH, P])
        w_dt = sb("w_dt", [P, DI])
        w_out = sb("w_out", [P, NH, P])
        w_ff1 = sb("w_ff1", [P, P])
        w_ff2 = sb("w_ff2", [P, P])
        w_xp = sb("w_xp", [P, P])
        w_gate = sb("w_gate", [P, P])
        w_c = sb("w_c", [P, P])
        w_d = sb("w_d", [P, P])
        w_y = sb("w_y", [P, P])
        w_sim = sb("w_sim", [P, SIM])
        ln_w = sb("ln_w", [P, P])
        ln_b = sb("ln_b", [P, P])
        gamma = sb("gamma", [P, P])
        beta = sb("beta", [P, P])
        rank_rev = sb("rank_rev", [P, SIM], BF16)
        decay = sb("decay", [P, NH, NS])
        norm_w = sb("norm_w", [P, 1])
        conv_b = sb("conv_b", [P, NH])
        dt_b = sb("dt_b", [P, NH])
        d_skip = sb("d_skip", [P, NH])
        b_ff1 = sb("b_ff1", [P, 1])
        b_ff2 = sb("b_ff2", [P, 1])
        b_xp = sb("b_xp", [P, 1])
        b_y = sb("b_y", [P, 1])
        b_xpy = sb("b_xpy", [P, 1])
        b_d = sb("b_d", [P, 1])
        b_gate = sb("b_gate", [P, 1])
        b_wb = sb("b_wb", [P, 1])
        b_bx = sb("b_bx", [P, 1])
        b_mat = sb("b_mat", [P, NS])
        eps = sb("eps", [P, 1])
        idle_dve = sb("idle_dve", [P, 1])

        x_in = sb("x_in", [P, NT, P])
        xn0 = [sb(f"xn0_{q}", [P, NT, P]) for q in range(2)]
        xr = sb("xr", [P, NT, P])
        xrT = sb("xrT", [P, NK - 1 + T])
        ucs = [sb(f"ucs{q}", [P, 2 * NH, T]) for q in range(2)]
        dbl = sb("dbl", [P, T])
        split = [sb(f"split{q}", [P, T], BF16) for q in range(2)]
        rest = sb("rest", [P, T])
        soft = sb("soft", [P, NH, T])
        delta = [sb(f"delta{q}", [P, NH, T]) for q in range(2)]
        du = [sb(f"du{q}", [P, NH, T]) for q in range(2)]
        st0, mv0 = sb("st0", [P, NT, 6]), sb("mv0", [P, NT, 2])
        ln0, rs0, m20, rr0, s20 = (sb(n, [P, NT]) for n in ("ln0", "rs0", "m20", "rr0", "s20"))

        dA = sb("dA", [P, NDA, NH, T])
        hp = sb("hp", [P, NP, NH, T])

        outT, outTb, h1T, x_res = (sb(n, [P, T]) for n in ("outT", "outTb", "h1T", "x_res"))
        stA, mvA, lnA, rsA = sb("stA", [P, NT, 6]), sb("mvA", [P, NT, 2]), sb("lnA", [P, NT]), sb("rsA", [P, NT])
        stB, mvB, lnB, rsB = sb("stB", [P, NT, 6]), sb("mvB", [P, NT, 2]), sb("lnB", [P, NT]), sb("rsB", [P, NT])
        stC, mvC, lnC, rsC = sb("stC", [P, NT, 6]), sb("mvC", [P, NT, 2]), sb("lnC", [P, NT]), sb("rsC", [P, NT])
        x1 = [sb(f"x1_{q}", [P, NT, P]) for q in range(2)]
        x2 = sb("x2", [P, NT, P])
        x3 = [sb(f"x3_{q}", [P, NT, P]) for q in range(2)]
        xnb = sb("xnb", [P, NT, P])
        xnbT = sb("xnbT", [P, T])
        xpT, xpTb, gates, hs = (sb(n, [P, T]) for n in ("xpT", "xpTb", "gates", "hs"))

        class Experts:

            def __init__(self, n):
                self.xn = sb(f"xn{n}", [P, NT, P])
                self.xnT = sb(f"xnT{n}", [P, T])
                self.mask = sb(f"mask{n}", [P, NT, SIM], BF16)
                self.rows = sb(f"rows{n}", [P, NT, HEADS, 2 * P])
                self.st, self.mv = sb(f"st{n}", [P, NT, 6]), sb(f"mv{n}", [P, NT, 2])
                self.ln, self.rs = sb(f"ln{n}", [P, NT]), sb(f"rs{n}", [P, NT])
                self.top = sb(f"top{n}", [P, NT, GR])
                self.rank = sb(f"rank{n}", [P, NT, GR])
                self.code = sb(f"code{n}", [P, NT, HEADS])
                self.score = sb(f"score{n}", [P, NT, HEADS])
                self.index = sb(f"index{n}", [P, NT, HEADS], U32)
                self.dot = sb(f"dot{n}", [P, NT, HEADS])
                self.act = sb(f"act{n}", [P, NT, HEADS])
                self.coef = sb(f"coef{n}", [P, NT, HEADS])
                self.mark = sb(f"mark{n}", [P, 1])
                self.started = sem(f"e{n}_started")
                self.stats = sem(f"e{n}_stats")
                self.logged = sem(f"e{n}_logged")
                self.rstd = sem(f"e{n}_rstd")
                self.normed = sem(f"e{n}_normed")
                self.turned = sem(f"e{n}_turned")
                self.turned_sb = sem(f"e{n}_turned_sb")
                self.sim = sem(f"e{n}_sim")
                self.topped = sem(f"e{n}_topped")
                self.masked = sem(f"e{n}_masked")
                self.picks = sem(f"e{n}_picks")
                self.indexed = sem(f"e{n}_indexed")
                self.fetched = [sem(f"e{n}_fetched{t}") for t in range(NT)]
                self.dotted = sem(f"e{n}_dotted")
                self.gelu = sem(f"e{n}_gelu")
                self.weighed = sem(f"e{n}_weighed")
                self.scaled = sem(f"e{n}_scaled")
                self.summed = sem(f"e{n}_summed")
                self.added = sem(f"e{n}_added")

        e1, e2 = Experts(1), Experts(2)

        bcast = [ctx.enter_context(nc.psum_tensor(f"bcast{k}", [P, 1, T], F32)) for k in range(NBC)]
        ysum = ctx.enter_context(nc.psum_tensor("ysum", [P, NH, T], F32))
        bank = [ctx.enter_context(nc.psum_tensor(f"bank{k}", [P, T], F32)) for k in range(3)]

        weights_in = sem("weights_in")
        cleared = sem("cleared")
        made = sem("made")
        folded = sem("folded")
        x_loaded = sem("x_loaded")
        p_stats = sem("p_stats")
        p_logged = sem("p_logged")
        p_rstd = sem("p_rstd")
        p_square = sem("p_square")
        p_scale = sem("p_scale")
        p_normed = sem("p_normed")
        p_turned = sem("p_turned")
        p_turned_sb = sem("p_turned_sb")
        conv_mm = sem("conv_mm")
        conv_sb = sem("conv_sb")
        silu_done = sem("silu_done")
        dbl_mm = sem("dbl_mm")
        dbl_sb = sem("dbl_sb")
        rest1 = sem("rest1")
        part2 = sem("part2")
        rest2 = sem("rest2")
        split_done = sem("split_done")
        dt_mm = sem("dt_mm")
        dt_sb = sem("dt_sb")
        dt_exp = sem("dt_exp")
        dt_log = sem("dt_log")
        delta_done = sem("delta_done")
        du_done = sem("du_done")
        decays = sem("decays")
        b_spread = sem("b_spread")
        c_spread = sem("c_spread")
        fed = sem("fed")
        scanned = sem("scanned")
        read_out = sem("read_out")
        y_sum = sem("y_sum")
        y_skip = sem("y_skip")
        y_gated = sem("y_gated")
        xres_loaded = sem("xres_loaded")
        a_out = sem("a_out")
        a_out_sb = sem("a_out_sb")
        a_h1 = sem("a_h1")
        a_h1_sb = sem("a_h1_sb")
        a_z = sem("a_z")
        a_stats = sem("a_stats")
        a_logged = sem("a_logged")
        a_rstd = sem("a_rstd")
        a_normed = sem("a_normed")
        a_affine = sem("a_affine")
        x1_done = sem("x1_done")
        b_stats = sem("b_stats")
        b_logged = sem("b_logged")
        b_rstd = sem("b_rstd")
        b_normed = sem("b_normed")
        c_stats = sem("c_stats")
        c_logged = sem("c_logged")
        c_rstd = sem("c_rstd")
        c_normed = sem("c_normed")
        b_turned = sem("b_turned")
        b_turned_sb = sem("b_turned_sb")
        b_xp_mm = sem("b_xp_mm")
        b_xp_sb = sem("b_xp_sb")
        b_gate_mm = sem("b_gate_mm")
        b_gate_sb = sem("b_gate_sb")
        b_fed = sem("b_fed")
        b_scanned = sem("b_scanned")
        b_y_mm = sem("b_y_mm")
        b_y_sb = sem("b_y_sb")
        b_z = sem("b_z")
        b_affine = sem("b_affine")
        x3_done = sem("x3_done")
        stored = sem("stored")

        tmp1 = e1.rows[:, 0, :, :].rearrange("p a b -> p (a b)")
        tmp2 = e1.rows[:, 1, :, :].rearrange("p a b -> p (a b)")
        tmp3 = e1.rows[:, 2, :, :].rearrange("p a b -> p (a b)")
        wq_t = tmp1[0:DK, 0:GR * P].rearrange("c (g d) -> c g d", g=GR)
        key_t = tmp2[0:DK, 0:SIM].rearrange("c (g k) -> c g k", g=GR)
        in_t = tmp2[:, 512:1024]
        wb_t = tmp2[:, 1024:1024 + P]
        taps = tmp3[:, 0:NK * DI].rearrange("p (k d) -> p k d", k=NK)
        rank_i = e1.rows[:, 3, 0:2, :].rearrange("p a b -> p (a b)").bitcast(I32)

        def everywhere(row):
            return row.partition_broadcast(P)

        loads = [
            (in_t, A["in_proj_t"]), (wq_t, A["wq_t"]), (key_t, A["key_t"]), (wb_t, A["wb_t"]),
            (taps.rearrange("p k d -> p (k d)"), everywhere(A["taps"])),
            (ln_w[:], everywhere(A["ln_w"])), (ln_b[:], everywhere(A["ln_b"])),
            (gamma[:], everywhere(A["gamma"])), (beta[:], everywhere(A["beta"])),
            (w_dt[DT0:DT0 + DR, :], A["dt_w_t"]), (w_out[:], A["out_t"]), (w_ff1[:], A["ff1_t"]),
            (w_ff2[:], A["ff2_t"]), (w_xp[:], A["W_in"]), (w_gate[:, IG:IG + NS], A["W_ig"]),
            (w_gate[:, FG:FG + NS], A["W_fg"]), (w_c[FG:FG + NS, :], A["C_mat"]), (w_d[:], A["W_D"]),
            (w_y[:], A["W_out"]), (decay[:], A["A_log"]), (norm_w[:], A["norm_w"]),
            (conv_b[:], A["conv_b"]), (dt_b[:], A["dt_b"]), (d_skip[:], A["Dp"]), (b_ff1[:], A["b1"]),
            (b_ff2[:], A["b2"]), (b_xp[:], A["b_in"]), (b_y[:], A["b_out"]), (b_d[:], A["b_D"]),
            (b_gate[IG:IG + NS, :], A["b_ig"]), (b_gate[FG:FG + NS, :], A["b_fg"]),
            (b_wb[:], A["b_B"]), (b_mat[:], A["B_mat"]),
            (w_xproj[:, :, DT0:DT0 + DR], A["xproj_t"][:, :, 0:DR]),
        ] + [(w_xproj[:, :, r:r + BC], A["xproj_t"][:, :, DR:DR + BC]) for r in PART]

        with nc.Block() as setup:
            @setup.sync
            def _(sp):
                sp.wait_ge(cleared, 1)
                for dst, src in loads:
                    sp.dma_start(dst, src).then_inc(weights_in, 16)

            @setup.gpsimd
            def _(pool):
                pool.memset(ident[:], 0.0).then_inc(made, 1)
                pool.wait_ge(made, 1)
                pool.affine_select(out=ident[:], in_=ident[:], compare_op=ALU.not_equal, fill=1.0, base=0,
                                   pattern=[[-1, P]], channel_multiplier=1).then_inc(made, 1)
                pool.iota(rank_i, pattern=[[0, GR], [-1, KEYS]], base=KEYS, channel_multiplier=0).then_inc(made, 1)

            @setup.vector
            def _(dve):
                for tile in (w_xproj, w_dt, w_gate, w_c, b_gate, hs, gates, dA, xrT, split[0], split[1], dbl):
                    nc.vector.memset(tile[:], 0.0)
                nc.vector.memset(eps[:], EPS).then_inc(cleared, 1)
                dve.wait_ge(made, 3)
                nc.vector.tensor_copy(rank_rev[:], rank_i)
                dve.wait_ge(cleared, 1)
                nc.vector.tensor_tensor(pick[:], ident[:, 0:BC], ident[:, PART[1]:PART[1] + BC],
                                        ALU.add).then_inc(cleared, 1)
                dve.wait_ge(cleared, 2)
                nc.vector.tensor_tensor(pick[:], pick[:], ident[:, PART[2]:PART[2] + BC], ALU.add)
                dve.wait_ge(weights_in, 16 * len(loads))
                nc.vector.tensor_scalar(in_t, in_t, norm_w[:, 0:1], None, ALU.mult).then_inc(cleared, 1)
                dve.wait_ge(cleared, 3)
                nc.vector.tensor_copy(w_res[:], in_t[:, DI:2 * DI])
                for k in range(NK):
                    nc.vector.tensor_tensor(w_taps[:, k, :], in_t[:, 0:DI], taps[:, k, :], ALU.mult)
                nc.vector.tensor_tensor(b_xpy[:], b_xp[:], b_y[:], ALU.add)
                dve.wait_ge(folded, 1)
                nc.vector.tensor_copy(w_sim[:], bank[0][:])
                nc.vector.tensor_copy(w_gate[:, BX:BX + NS], bank[1][:, 0:NS])
                nc.vector.tensor_copy(b_bx[0:NS, :], bank[1][0:NS, NS:NS + 1]).then_inc(cleared, 1)

            @setup.scalar
            def _(act):
                act.wait_ge(weights_in, 16 * len(loads))
                nc.scalar.activation(decay[:], decay[:], ACT.Exp).then_inc(p_scale, 1)
                act.wait_ge(p_scale, 1)
                nc.scalar.mul(decay[:], decay[:], -1.0).then_inc(p_scale, 1)

            @setup.tensor
            def _(pe):
                pe.wait_ge(weights_in, 16 * len(loads))
                for g in range(GR):
                    nc.tensor.matmul(bank[0][:, g * KEYS:(g + 1) * KEYS], wq_t[:, g, :], key_t[:, g, :],
                                     start=True, stop=True, skip_group_check=True)
                nc.tensor.matmul(bank[1][:, 0:NS], wb_t, b_mat[:], start=True, stop=True, skip_group_check=True)
                nc.tensor.matmul(bank[1][0:NS, NS:NS + 1], b_mat[:], b_wb[:], start=True, stop=True,
                                 skip_group_check=True).then_inc(folded, 1)

        P_SCALE0 = 2

        block = ctx.enter_context(nc.Block())

        @block.sync
        def _(sp):
            def iteration(i, q, has):
                b = {p: i + o for p, o in OFFSET.items()}
                if PRE in has:
                    n = b[PRE]
                    if later(n):
                        sp.wait_ge(p_normed, at(n - 1, 1))
                    sp.dma_start(x_in[:], A["x"][n]).then_inc(x_loaded, 16)
                if PA in has:
                    n = b[PA]
                    if later(n):
                        sp.wait_ge(x1_done, at(n - 1, 1))
                    sp.dma_start(x_res[:].rearrange("p (a d) -> p a d", a=NT), A["x"][n]).then_inc(xres_loaded, 16)
                if PD in has:
                    n = b[PD]
                    sp.wait_ge(e2.added, at(n, 1))
                    sp.dma_start(A["y"][n], x3[q][:]).then_inc(stored, 16)

            run_pipeline(sp, iteration)
            sp.wait_ge(stored, 16 * NB)

        @block.tensor
        def _(pe):
            busy = {}

            def claim(k, i):
                if k in busy:
                    s, per, nth, off = busy[k]
                    pe.wait_ge(s, at(i + off, per, nth))

            def turn(k, i, src, s):
                for t in range(NT):
                    mm = nc.tensor.transpose(bank[k][:, t * P:(t + 1) * P], src[:, t, :], ident[:])
                mm.then_inc(s, 1)

            def experts_sim(e, k, i, off, t):
                claim(k, i)
                if t == 0:
                    pe.wait_ge(e.turned_sb, at(i + off, 1))
                nc.tensor.matmul(bank[k][:], e.xnT[:, t * P:(t + 1) * P], w_sim[:], start=True,
                                 stop=True).then_inc(e.sim, 1)
                busy[k] = (e.masked, NT, t, off)

            def experts_sum(e, k, i, off):
                claim(k, i)
                pe.wait_ge(e.scaled, at(i + off, NT, NT - 1))
                for h in range(HEADS):
                    mm = nc.tensor.matmul(bank[k][:].rearrange("p (t d) -> p t d", t=NT), ident[:],
                                          e.rows[:, :, h, P:2 * P], start=(h == 0), stop=(h == HEADS - 1))
                mm.then_inc(e.summed, 1)
                busy[k] = (e.added, 1, 0, off)

            def iteration(i, q, has):
                for k in busy:
                    s, per, nth, off = busy[k]
                    busy[k] = (s, per, nth, off - 1)
                b = {p: i + o for p, o in OFFSET.items()}

                def spread(c, part, n):
                    if n == 0:
                        pe.wait_ge(split_done, at(c, 1))
                    for w, s in enumerate((b_spread, c_spread)):
                        k = 2 * n + w
                        if k >= NBC:
                            pe.wait_ge((fed, read_out)[(k - NBC) % 2], at(c, NS, (k - NBC) // 2))
                        elif later(c):
                            last = max(x for x in range(2 * NS) if x % NBC == k)
                            pe.wait_ge((fed, read_out)[last % 2], at(c - 1, NS, last // 2))
                        r = w * NS + n
                        nc.tensor.matmul(bcast[k % NBC][:, 0, :], pick[:, r:r + 1].to_broadcast([P, P]), part[:],
                                         start=True, stop=True).then_inc(s, 1)

                for n in range(NS):
                    if CORE in has:
                        c = b[CORE]
                        if n + 1 < NS:
                            spread(c, split[q], n + 1)
                        if n == 0 and later(c):
                            pe.wait_ge(y_skip, at(c - 1, 1))
                        pe.wait_ge(read_out, at(c, NS, n))
                        for j in range(NH):
                            mm = nc.tensor.matmul(ysum[:, j, :], ident[:], hp[:, n % NP, j, :],
                                                  start=(n == 0), stop=(n == NS - 1))
                        mm.then_inc(y_sum, 1)
                    if PRE in has:
                        p = b[PRE]
                        if n == 4:
                            claim(0, i)
                            pe.wait_ge(p_normed, at(p, 1))
                            turn(0, i, xr, p_turned)
                            busy[0] = (p_turned_sb, 1, 0, OFFSET[PRE])
                        if 5 <= n < 7:
                            j = n - 5
                            claim(0, i)
                            if j == 0:
                                pe.wait_ge(p_turned_sb, at(p, 1))
                            for k in range(NK):
                                mm = nc.tensor.matmul(bank[0][:], w_taps[:, k, j * P:(j + 1) * P], xrT[:, k:k + T],
                                                      start=(k == 0), stop=(k == NK - 1))
                            mm.then_inc(conv_mm, 1)
                            busy[0] = (conv_sb, 2 * NH, j, OFFSET[PRE])
                        if 7 <= n < 9:
                            j = n - 7
                            claim(0, i)
                            nc.tensor.matmul(bank[0][:], w_res[:, j * P:(j + 1) * P], xrT[:, NK - 1:NK - 1 + T],
                                             start=True, stop=True).then_inc(conv_mm, 1)
                            busy[0] = (conv_sb, 2 * NH, NH + j, OFFSET[PRE])
                        if n == 9:
                            claim(0, i)
                            pe.wait_ge(silu_done, at(p, 1))
                            for j in range(NH):
                                mm = nc.tensor.matmul(bank[0][:], w_xproj[:, j, :], ucs[1 - q][:, j, :],
                                                      start=(j == 0), stop=(j == NH - 1))
                            mm.then_inc(dbl_mm, 1)
                            busy[0] = (dbl_sb, 1, 0, OFFSET[PRE])
                        if 10 <= n < 12:
                            j = n - 10
                            claim(0, i)
                            if j == 0:
                                pe.wait_ge(dbl_sb, at(p, 1))
                            nc.tensor.matmul(bank[0][:], w_dt[:, j * P:(j + 1) * P], dbl[:], start=True,
                                             stop=True).then_inc(dt_mm, 1)
                            busy[0] = (dt_sb, NH, j, OFFSET[PRE])
                        if n == NS - 1:
                            spread(p, split[1 - q], 0)
                    if PA in has:
                        a = b[PA]
                        if n == 0:
                            claim(1, i)
                            pe.wait_ge(y_gated, at(a, 1))
                            for j in range(NH):
                                nc.tensor.matmul(bank[1][:], w_out[:, j, :], ucs[1 - q][:, j, :], start=(j == 0),
                                                 stop=False, skip_group_check=True)
                            for t in range(NT):
                                mm = nc.tensor.matmul(bank[1][:, t * P:(t + 1) * P], xn0[1 - q][:, t, :], ident[:],
                                                      start=False, stop=True, skip_group_check=True)
                            mm.then_inc(a_out, 1)
                            busy[1] = (a_out_sb, 1, 0, OFFSET[PA])
                        if n == 1:
                            claim(1, i)
                            pe.wait_ge(a_out_sb, at(a, 1))
                            nc.tensor.matmul(bank[1][:], w_ff1[:], outT[:], start=True, stop=True).then_inc(a_h1, 1)
                            busy[1] = (a_h1_sb, 1, 0, OFFSET[PA])
                        if n == 2:
                            claim(1, i)
                            pe.wait_ge(a_h1_sb, at(a, 1))
                            for t in range(NT):
                                tok = slice(t * P, (t + 1) * P)
                                nc.tensor.matmul(bank[1][:, tok], h1T[:, tok], w_ff2[:], start=True, stop=False,
                                                 skip_group_check=True)
                                mm = nc.tensor.matmul(bank[1][:, tok], outTb[:, tok], ident[:], start=False,
                                                      stop=True, skip_group_check=True)
                            mm.then_inc(a_z, 1)
                            busy[1] = (a_normed, 1, 0, OFFSET[PA])
                        if n == 7:
                            claim(1, i)
                            pe.wait_ge(e1.normed, at(a, 1))
                            turn(1, i, e1.xn, e1.turned)
                            busy[1] = (e1.turned_sb, 1, 0, OFFSET[PA])
                        if 8 <= n < 8 + NT:
                            experts_sim(e1, 1, i, OFFSET[PA], n - 8)
                    if PC in has:
                        m = b[PC]
                        if n == 2:
                            claim(2, i)
                            pe.wait_ge(b_y_sb, at(m, 1))
                            for t in range(NT):
                                tok = slice(t * P, (t + 1) * P)
                                nc.tensor.matmul(bank[2][:, tok], xnbT[:, tok], w_y[:], start=True, stop=False,
                                                 skip_group_check=True)
                                mm = nc.tensor.matmul(bank[2][:, tok], xpTb[:, tok], ident[:], start=False,
                                                      stop=True, skip_group_check=True)
                            mm.then_inc(b_z, 1)
                            busy[2] = (c_normed, 1, 0, OFFSET[PC])
                        if n == 12:
                            claim(0, i)
                            pe.wait_ge(e2.normed, at(m, 1))
                            turn(0, i, e2.xn, e2.turned)
                            busy[0] = (e2.turned_sb, 1, 0, OFFSET[PC])
                        if 13 <= n:
                            experts_sim(e2, 0, i, OFFSET[PC], n - 13)
                    if PB in has:
                        m = b[PB]
                        if n == 8:
                            experts_sum(e1, 2, i, OFFSET[PB])
                        if n == 11:
                            claim(2, i)
                            pe.wait_ge(b_normed, at(m, 1))
                            turn(2, i, xnb, b_turned)
                            busy[2] = (b_turned_sb, 1, 0, OFFSET[PB])
                        if n == 12:
                            claim(2, i)
                            pe.wait_ge(b_turned_sb, at(m, 1))
                            nc.tensor.matmul(bank[2][:], w_xp[:], xnbT[:], start=True, stop=True).then_inc(b_xp_mm, 1)
                            busy[2] = (b_xp_sb, 1, 0, OFFSET[PB])
                        if n == 13:
                            claim(2, i)
                            pe.wait_ge(b_xp_sb, at(m, 1))
                            nc.tensor.matmul(bank[2][:], w_gate[:], xpT[:], start=True, stop=True).then_inc(b_gate_mm, 1)
                            busy[2] = (b_fed, 1, 0, OFFSET[PB])
                        if n == 14:
                            claim(2, i)
                            nc.tensor.matmul(bank[2][:], w_d[:], xpT[:], start=True, stop=False)
                            pe.wait_ge(b_scanned, at(m, 1))
                            nc.tensor.matmul(bank[2][:], w_c[:], hs[:], start=False, stop=True).then_inc(b_y_mm, 1)
                            busy[2] = (b_y_sb, 1, 0, OFFSET[PB])
                    if PD in has:
                        if n == 0:
                            experts_sim(e2, 0, i, OFFSET[PD], NT - 1)
                        if n == 13:
                            experts_sum(e2, 1, i, OFFSET[PD])

            run_pipeline(pe, iteration)

        @block.scalar
        def _(act):
            act.preload_act_table_set(EXP_AND_LN)

            def inverse_root(var, ln, out, logged, ln_at, done):
                nc.scalar.activation(ln[:], var, ACT.Ln, bias=eps[:, 0:1]).then_inc(logged, 1)
                act.wait_ge(logged, ln_at)
                nc.scalar.activation(out[:], ln[:], ACT.Exp, scale=-0.5).then_inc(done, 1)

            def experts_rstd(e, n):
                act.wait_ge(e.stats, at(n, 2, 1))
                inverse_root(e.mv[:, :, 1], e.ln, e.rs, e.logged, at(n, 1), e.rstd)

            def experts_turned(e, k, n):
                act.wait_ge(e.turned, at(n, 1))
                nc.scalar.activation(e.xnT[:], bank[k][:], ACT.Copy).then_inc(e.turned_sb, 1)

            def experts_gelu(e, n):
                act.wait_ge(e.dotted, at(n, NT, NT - 1))
                nc.scalar.activation(e.act[:], e.dot[:], ACT.Gelu).then_inc(e.gelu, 1)
                act.preload_act_table_set(EXP_AND_LN)

            def experts_scale(e, n, t):
                if t == 0:
                    act.wait_ge(e.weighed, at(n, 1))
                for h in range(HEADS):
                    row = e.rows[:, t, h, P:2 * P]
                    op = nc.scalar.activation(row, row, ACT.Copy, scale=e.coef[:, t, h:h + 1])
                op.then_inc(e.scaled, 1)

            def iteration(i, q, has):
                b = {p: i + o for p, o in OFFSET.items()}

                def decays_of(n):
                    c = b[CORE]
                    if n == 0:
                        act.wait_ge(delta_done, at(c, 1))
                    if n >= NDA:
                        act.wait_ge(scanned, at(c, NS, n - NDA))
                    elif later(c):
                        act.wait_ge(scanned, at(c - 1, NS, NS + n - NDA))
                    for j in range(NH):
                        op = nc.scalar.activation(dA[:, n % NDA, j, 1:T], delta[q][:, j, 1:T], ACT.Exp,
                                                  scale=decay[:, j, n:n + 1])
                    op.then_inc(decays, 1)

                for n in range(NS):
                    if CORE in has:
                        for m in range(LEAD + 1) if n == 0 else [n + LEAD] if n + LEAD < NS else []:
                            decays_of(m)
                    if PA in has:
                        a = b[PA]
                        if n == 1:
                            act.wait_ge(a_out, at(a, 1))
                            if later(a):
                                act.wait_ge(x1_done, at(a - 1, 1))
                            nc.scalar.activation(outT[:], bank[1][:], ACT.Copy)
                            nc.scalar.activation(outTb[:], bank[1][:], ACT.Identity,
                                                 bias=b_ff2[:, 0:1]).then_inc(a_out_sb, 1)
                    if PC in has and n == 2:
                        m = b[PC]
                        act.wait_ge(b_y_mm, at(m, 1))
                        nc.scalar.activation(xnbT[:], bank[2][:], ACT.Tanh, bias=b_d[:, 0:1]).then_inc(b_y_sb, 1)
                    if PA in has:
                        if n == 2:
                            act.wait_ge(a_h1, at(a, 1))
                            nc.scalar.activation(h1T[:], bank[1][:], ACT.Gelu, bias=b_ff1[:, 0:1]).then_inc(a_h1_sb, 1)
                            act.preload_act_table_set(EXP_AND_LN)
                        if n == 4:
                            act.wait_ge(a_stats, at(a, 2, 1))
                            inverse_root(mvA[:, :, 1], lnA, rsA, a_logged, at(a, 1), a_rstd)
                        if n == 7:
                            experts_rstd(e1, a)
                        if n == 8:
                            experts_turned(e1, 1, a)
                    elif n == 2 and PC in has:
                        act.preload_act_table_set(EXP_AND_LN)
                    if PRE in has:
                        p = b[PRE]
                        if n == 2:
                            act.wait_ge(p_stats, at(p, 2, 1))
                            inverse_root(mv0[:, :, 1], ln0, rs0, p_logged, at(p, 2, 0), p_rstd)
                        if n == 3:
                            act.wait_ge(p_square, at(p, 2, 1))
                            inverse_root(m20[:], ln0, rr0, p_logged, at(p, 2, 1), p_rstd)
                        if n == 5:
                            act.wait_ge(p_turned, at(p, 1))
                            nc.scalar.activation(xrT[:, NK - 1:NK - 1 + T], bank[0][:], ACT.Copy)\
                                .then_inc(p_turned_sb, 1)
                        if 6 <= n < 6 + 2 * NH:
                            j = n - 6
                            act.wait_ge(conv_mm, at(p, 2 * NH, j))
                            if j == 0 and second(p):
                                act.wait_ge(a_out, at(p - 2, 1))
                            if j < NH:
                                op = nc.scalar.activation(ucs[1 - q][:, j, :], bank[0][:], ACT.Identity,
                                                          bias=conv_b[:, j:j + 1])
                            else:
                                op = nc.scalar.activation(ucs[1 - q][:, j, :], bank[0][:], ACT.Copy)
                            op.then_inc(conv_sb, 1)
                        if n == 9:
                            act.wait_ge(conv_sb, at(p, 2 * NH, 2 * NH - 1))
                            nc.scalar.activation(ucs[1 - q][:], ucs[1 - q][:], ACT.Silu).then_inc(silu_done, 1)
                            act.preload_act_table_set(EXP_AND_LN)
                        if n == 10:
                            act.wait_ge(dbl_mm, at(p, 1))
                            nc.scalar.activation(dbl[:], bank[0][:], ACT.Copy)
                            nc.scalar.activation(split[1 - q][:], bank[0][:], ACT.Copy).then_inc(dbl_sb, 1)
                        if 11 <= n < 13:
                            j = n - 11
                            act.wait_ge(dt_mm, at(p, NH, j))
                            if j == 0 and later(p):
                                act.wait_ge(delta_done, at(p - 1, 1))
                            nc.scalar.activation(soft[:, j, :], bank[0][:], ACT.Abs, bias=dt_b[:, j:j + 1])
                            nc.scalar.activation(delta[1 - q][:, j, :], bank[0][:], ACT.Relu,
                                                 bias=dt_b[:, j:j + 1]).then_inc(dt_sb, 1)
                        if n == 11:
                            act.wait_ge(rest1, at(p, 1))
                            nc.scalar.activation(split[1 - q][PART[1]:, :], rest[PART[1]:, :], ACT.Copy)\
                                .then_inc(part2, 1)
                        if n == 12:
                            act.wait_ge(rest2, at(p, 1))
                            nc.scalar.activation(split[1 - q][PART[2]:, :], rest[PART[2]:, :], ACT.Copy)\
                                .then_inc(split_done, 1)
                            act.wait_ge(dt_sb, at(p, NH, NH - 1))
                            nc.scalar.activation(soft[:], soft[:], ACT.Exp, scale=-1.0).then_inc(dt_exp, 1)
                        if n == 13:
                            act.wait_ge(dt_exp, at(p, 1))
                            nc.scalar.activation(soft[:], soft[:], ACT.Ln, bias=1.0).then_inc(dt_log, 1)
                    if PB in has:
                        m = b[PB]
                        if n == 5:
                            experts_gelu(e1, m)
                        if n in (6, 7):
                            for t in range(2 * (n - 6), 2 * (n - 6) + 2):
                                experts_scale(e1, m, t)
                        if n == 11:
                            act.wait_ge(b_stats, at(m, 2, 1))
                            inverse_root(mvB[:, :, 1], lnB, rsB, b_logged, at(m, 1), b_rstd)
                        if n == 12:
                            act.wait_ge(b_turned, at(m, 1))
                            nc.scalar.activation(xnbT[:], bank[2][:], ACT.Copy).then_inc(b_turned_sb, 1)
                        if n == 13:
                            act.wait_ge(b_xp_mm, at(m, 1))
                            nc.scalar.activation(xpT[:], bank[2][:], ACT.Identity, bias=b_xp[:, 0:1])
                            nc.scalar.activation(xpTb[:], bank[2][:], ACT.Identity,
                                                 bias=b_xpy[:, 0:1]).then_inc(b_xp_sb, 1)
                        if n == 14:
                            act.wait_ge(b_gate_mm, at(m, 1))
                            nc.scalar.activation(gates[0:FG + NS, :], bank[2][0:FG + NS, :], ACT.Sigmoid,
                                                 bias=b_gate[0:FG + NS, 0:1]).then_inc(b_gate_sb, 1)
                            act.preload_act_table_set(EXP_AND_LN)
                    if PC in has:
                        m = b[PC]
                        if n == 4:
                            act.wait_ge(c_stats, at(m, 2, 1))
                            inverse_root(mvC[:, :, 1], lnC, rsC, c_logged, at(m, 1), c_rstd)
                        if n == 11:
                            experts_rstd(e2, m)
                        if n == 13:
                            experts_turned(e2, 0, m)
                    if PD in has:
                        if n == 11:
                            experts_gelu(e2, b[PD])
                        if n in (12, 13):
                            for t in range(2 * (n - 12), 2 * (n - 12) + 2):
                                experts_scale(e2, b[PD], t)

            run_pipeline(act, iteration)

        @block.vector
        def _(dve):
            def statistics(src, st, mv, s, base):
                for t in range(NT):
                    op = nc.vector.bn_stats(st[:, t, :], src[:, t, :])
                op.then_inc(s, 1)
                dve.wait_ge(s, base)
                nc.vector.memset(idle_dve[:], 0.0)
                for t in range(NT):
                    op = nc.vector.bn_aggr(mv[:, t, :], st[:, t, :])
                op.then_inc(s, 1)

            def normalise(dst, src, mv, scale, s):
                for t in range(NT):
                    op = nc.vector.tensor_scalar(dst[:, t, :], src[:, t, :], mv[:, t, 0:1], scale[:, t:t + 1],
                                                 ALU.subtract, ALU.mult)
                if s is not None:
                    op.then_inc(s, 1)

            def tokens(k):
                return bank[k][:].rearrange("p (t d) -> p t d", t=NT)

            def experts_top(e, k, n, t):
                dve.wait_ge(e.sim, at(n, NT, t))
                sims = bank[k][:].rearrange("p (g k) -> p g k", g=GR)
                nc.vector.tensor_reduce(e.top[:, t, :], sims, AX_X, ALU.max).then_inc(e.topped, 1)
                dve.wait_ge(e.topped, at(n, NT, t))
                nc.vector.tensor_tensor(e.mask[:, t, :].rearrange("p (g k) -> p g k", g=GR), sims,
                                        e.top[:, t, :].unsqueeze(2).to_broadcast([P, GR, KEYS]),
                                        ALU.is_equal).then_inc(e.masked, 1)

            def experts_index(e, n):
                dve.wait_ge(e.masked, at(n, NT, NT - 1))
                nc.vector.tensor_tensor(e.mask[:], e.mask[:], rank_rev[:].unsqueeze(1).to_broadcast([P, NT, SIM]),
                                        ALU.mult).then_inc(e.picks, 1)
                dve.wait_ge(e.picks, at(n, 3, 0))
                nc.vector.tensor_reduce(e.rank[:], e.mask[:].rearrange("p t (g k) -> p t g k", g=GR), AX_X,
                                        ALU.max).then_inc(e.picks, 1)
                dve.wait_ge(e.picks, at(n, 3, 1))
                nc.vector.scalar_tensor_tensor(out=e.code[:], in0=e.rank[:, :, 0:HEADS], scalar=-float(KEYS),
                                               in1=e.rank[:, :, HEADS:GR], op0=ALU.mult,
                                               op1=ALU.subtract).then_inc(e.picks, 1)
                dve.wait_ge(e.picks, at(n, 3, 2))
                nc.vector.tensor_tensor(e.score[:], e.top[:, :, 0:HEADS], e.top[:, :, HEADS:GR], ALU.add)
                nc.vector.tensor_scalar(e.index[:], e.code[:], float(KEYS * KEYS + KEYS), None,
                                        ALU.add).then_inc(e.indexed, 1)

            def experts_dot(e, n, t):
                dve.wait_ge(e.fetched[t], (n + 1) * (16 * HEADS))
                for h in range(HEADS):
                    row = e.rows[:, t, h, 0:P]
                    op = nc.vector.tensor_tensor_reduce(row, row, e.xn[:, t, :], 1.0, 0.0, ALU.mult, ALU.add,
                                                        e.dot[:, t, h:h + 1])
                op.then_inc(e.dotted, 1)

            def experts_weigh(e, n):
                dve.wait_ge(e.gelu, at(n, 1))
                nc.vector.scalar_tensor_tensor(out=e.coef[:], in0=e.score[:], scalar=0.0, in1=e.act[:], op0=ALU.max,
                                               op1=ALU.mult).then_inc(e.weighed, 1)

            def iteration(i, q, has):
                b = {p: i + o for p, o in OFFSET.items()}
                for n in range(NS):
                    if CORE in has:
                        c = b[CORE]
                        state = hp[:, n % NP, :, :]
                        flat = state.rearrange("p a b -> p (a b)")
                        if n == 0:
                            dve.wait_ge(du_done, at(c, 1))
                        dve.wait_ge(b_spread, at(c, NS, n))
                        if n >= NP:
                            dve.wait_ge(y_sum, at(c, NS, n - NP))
                        elif later(c):
                            dve.wait_ge(y_sum, at(c - 1, NS, NS + n - NP))
                        nc.vector.tensor_tensor(state, du[q][:],
                                                bcast[2 * n % NBC][:].to_broadcast([P, NH, T]),
                                                ALU.mult).then_inc(fed, 1)
                        dve.wait_ge(decays, at(c, NS, n))
                        dve.wait_ge(fed, at(c, NS, n))
                        nc.vector.tensor_tensor_scan(flat, dA[:, n % NDA, :, :].rearrange("p a b -> p (a b)"), flat,
                                                     0.0, ALU.mult, ALU.add).then_inc(scanned, 1)
                        dve.wait_ge(c_spread, at(c, NS, n))
                        dve.wait_ge(scanned, at(c, NS, n))
                        nc.vector.tensor_tensor(state, state,
                                                bcast[(2 * n + 1) % NBC][:].to_broadcast([P, NH, T]),
                                                ALU.mult).then_inc(read_out, 1)
                    if PC in has:
                        m = b[PC]
                        if n == 3:
                            dve.wait_ge(b_z, at(m, 1))
                            statistics(tokens(2), stC, mvC, c_stats, at(m, 2, 0))
                        if n == 4:
                            dve.wait_ge(c_rstd, at(m, 1))
                            normalise(xnb, tokens(2), mvC, rsC, c_normed)
                        if n == 10:
                            dve.wait_ge(x3_done, at(m, 1))
                            statistics(x3[1 - q], e2.st, e2.mv, e2.stats, at(m, 2, 0))
                        if n == 11:
                            dve.wait_ge(e2.rstd, at(m, 1))
                            normalise(e2.xn, x3[1 - q], e2.mv, e2.rs, e2.normed)
                        if 14 <= n:
                            experts_top(e2, 0, m, n - 14)
                    if PA in has:
                        a = b[PA]
                        if n == 3:
                            dve.wait_ge(a_z, at(a, 1))
                            statistics(tokens(1), stA, mvA, a_stats, at(a, 2, 0))
                        if n == 4:
                            dve.wait_ge(a_rstd, at(a, 1))
                            normalise(outT[:].rearrange("p (t d) -> p t d", t=NT), tokens(1), mvA, rsA, a_normed)
                        if n == 6:
                            dve.wait_ge(x1_done, at(a, 1))
                            statistics(x1[1 - q], e1.st, e1.mv, e1.stats, at(a, 2, 0))
                        if n == 7:
                            dve.wait_ge(e1.rstd, at(a, 1))
                            normalise(e1.xn, x1[1 - q], e1.mv, e1.rs, e1.normed)
                        if 9 <= n < 9 + NT:
                            experts_top(e1, 1, a, n - 9)
                        if n == 12:
                            experts_index(e1, a)
                    if PRE in has:
                        p = b[PRE]
                        if n == 1:
                            dve.wait_ge(x_loaded, (p + 1) * 16)
                            statistics(x_in, st0, mv0, p_stats, at(p, 2, 0))
                        if n == 2:
                            dve.wait_ge(p_rstd, at(p, 2, 0))
                            nc.vector.tensor_tensor(m20[:], mv0[:, :, 1], rs0[:], ALU.mult).then_inc(p_square, 1)
                            dve.wait_ge(p_square, at(p, 2, 0))
                            nc.vector.tensor_tensor(m20[:], m20[:], rs0[:], ALU.mult).then_inc(p_square, 1)
                        if n == 3:
                            dve.wait_ge(p_rstd, at(p, 2, 1))
                            nc.vector.tensor_tensor(s20[:], rs0[:], rr0[:], ALU.mult).then_inc(p_scale, 1)
                            if second(p):
                                dve.wait_ge(a_out, at(p - 2, 1))
                            normalise(xn0[1 - q], x_in, mv0, rs0, None)
                            dve.wait_ge(p_scale, P_SCALE0 + at(p, 1))
                            if later(p):
                                dve.wait_ge(p_turned, at(p - 1, 1))
                            normalise(xr, x_in, mv0, s20, p_normed)
                    if PB in has:
                        m = b[PB]
                        if n in (2, 3):
                            experts_dot(e1, m, 2 * (n - 2))
                            experts_dot(e1, m, 2 * (n - 2) + 1)
                        if n == 5:
                            experts_weigh(e1, m)
                        if n == 10:
                            dve.wait_ge(e1.summed, at(m, 1))
                            nc.vector.tensor_tensor(x2[:], tokens(2), x1[q][:], ALU.add).then_inc(e1.added, 1)
                            dve.wait_ge(e1.added, at(m, 1))
                            statistics(x2, stB, mvB, b_stats, at(m, 2, 0))
                        if n == 11:
                            dve.wait_ge(b_rstd, at(m, 1))
                            if later(m):
                                dve.wait_ge(x3_done, at(m - 1, 1))
                            normalise(xnb, x2, mvB, rsB, b_normed)
                        if n == 14:
                            dve.wait_ge(b_gate_sb, at(m, 1))
                            nc.vector.scalar_tensor_tensor(out=hs[FG:FG + NS, :], in0=bank[2][BX:BX + NS, :],
                                                           scalar=b_bx[0:NS, 0:1], in1=gates[IG:IG + NS, :],
                                                           op0=ALU.add, op1=ALU.mult).then_inc(b_fed, 1)
                            dve.wait_ge(b_fed, at(m, 1))
                            nc.vector.tensor_tensor_scan(hs[FG:FG + NS, :], gates[FG:FG + NS, :], hs[FG:FG + NS, :],
                                                         0.0, ALU.mult, ALU.add).then_inc(b_scanned, 1)
                    if PD in has:
                        g = b[PD]
                        if n == 0:
                            experts_top(e2, 0, g, NT - 2)
                        if n == 1:
                            experts_top(e2, 0, g, NT - 1)
                            experts_index(e2, g)
                        if n in (8, 9):
                            experts_dot(e2, g, 2 * (n - 8))
                            experts_dot(e2, g, 2 * (n - 8) + 1)
                        if n == 11:
                            experts_weigh(e2, g)
                        if n == NS - 1:
                            dve.wait_ge(e2.summed, at(g, 1))
                            nc.vector.tensor_tensor(x3[q][:], tokens(1), x3[q][:], ALU.add).then_inc(e2.added, 1)
                if CORE in has:
                    c = b[CORE]
                    dve.wait_ge(y_sum, at(c, NS, NS - 1))
                    for j in range(NH):
                        op = nc.vector.scalar_tensor_tensor(out=ucs[q][:, j, :], in0=ucs[q][:, j, :],
                                                            scalar=d_skip[:, j:j + 1], in1=ysum[:, j, :],
                                                            op0=ALU.mult, op1=ALU.add)
                    op.then_inc(y_skip, 1)
                    dve.wait_ge(y_skip, at(c, 1))
                    nc.vector.tensor_tensor(ucs[q][:, 0:NH, :], ucs[q][:, 0:NH, :], ucs[q][:, NH:2 * NH, :],
                                            ALU.mult).then_inc(y_gated, 1)

            run_pipeline(dve, iteration)

        @block.gpsimd
        def _(pool):
            def fetch(e, n, t):
                if t == 0:
                    pool.wait_ge(e.indexed, at(n, 1))
                    if later(n):
                        pool.wait_ge(e.summed, at(n - 1, 1))
                        pool.wait_ge(e.started, at(n - 1, 1))
                    pool.tensor_tensor(e.mark[:], eps[:], eps[:], ALU.add).then_inc(e.started, 1)
                for h in range(HEADS):
                    pool.indirect_dma_start(
                        e.rows[:, t, h, :], None, A["experts"],
                        bass.IndirectOffsetOnAxis(ap=e.index[:, t, h:h + 1], axis=0)).then_inc(e.fetched[t], 16)

            def affine(rows, scale, shift, s, n):
                pool.tensor_tensor(rows, rows, scale[:].unsqueeze(1).to_broadcast([P, NT, P]),
                                   ALU.mult).then_inc(s, 1)
                pool.wait_ge(s, at(n, 2, 0))
                pool.tensor_tensor(rows, rows, shift[:].unsqueeze(1).to_broadcast([P, NT, P]),
                                   ALU.add).then_inc(s, 1)
                pool.wait_ge(s, at(n, 2, 1))

            def iteration(i, q, has):
                b = {p: i + o for p, o in OFFSET.items()}
                for n in range(NS):
                    if PD in has and n in (1, 2):
                        fetch(e2, b[PD], n - 1)
                    if PA in has and n == 4:
                        a = b[PA]
                        z = outT[:].rearrange("p (t d) -> p t d", t=NT)
                        pool.wait_ge(xres_loaded, (a + 1) * 16)
                        pool.wait_ge(a_normed, at(a, 1))
                        affine(z, ln_w, ln_b, a_affine, a)
                        if second(a):
                            pool.wait_ge(e1.added, at(a - 2, 1))
                        pool.tensor_tensor(x1[1 - q][:], z, x_res[:].rearrange("p (t d) -> p t d", t=NT),
                                           ALU.add).then_inc(x1_done, 1)
                    if PD in has and n == 5:
                        fetch(e2, b[PD], 2)
                    if PC in has and n == 6:
                        m = b[PC]
                        pool.wait_ge(c_normed, at(m, 1))
                        affine(xnb[:], gamma, beta, b_affine, m)
                        if second(m):
                            pool.wait_ge(stored, (m - 1) * 16)
                        pool.tensor_tensor(x3[1 - q][:], xnb[:], x2[:], ALU.add).then_inc(x3_done, 1)
                    if PD in has and n == 7:
                        fetch(e2, b[PD], 3)
                    if PRE in has and n == 11:
                        p = b[PRE]
                        pool.wait_ge(dbl_sb, at(p, 1))
                        pool.tensor_tensor(rest[:], dbl[:], split[1 - q][:], ALU.subtract).then_inc(rest1, 1)
                        pool.wait_ge(part2, at(p, 1))
                        pool.tensor_tensor(rest[:], rest[:], split[1 - q][:], ALU.subtract).then_inc(rest2, 1)
                    if PA in has and n == 12:
                        fetch(e1, b[PA], 0)
                    if PRE in has and n == 13:
                        p = b[PRE]
                        pool.wait_ge(dt_log, at(p, 1))
                        pool.tensor_tensor(delta[1 - q][:], delta[1 - q][:], soft[:], ALU.add).then_inc(delta_done, 1)
                        pool.wait_ge(delta_done, at(p, 1))
                        if second(p):
                            pool.wait_ge(fed, at(p - 2, NS, NS - 1))
                        pool.tensor_tensor(du[1 - q][:], delta[1 - q][:], ucs[1 - q][:, 0:NH, :],
                                           ALU.mult).then_inc(du_done, 1)
                    if PA in has and n > 12:
                        fetch(e1, b[PA], n - 12)

            run_pipeline(pool, iteration)


def kernel(**inputs):
    import numpy as np
    import concourse.bacc as bacc
    from concourse.bass_utils import run_bass_kernel_spmd

    def a(name):
        return np.asarray(inputs["L0_attn_a_" + name])

    def b(name):
        return np.asarray(inputs["L0_attn_b_" + name])

    def f(name):
        return np.asarray(inputs["L0_ffn_" + name])

    def halves(v):
        return v.reshape(NH, P, -1).transpose(1, 0, 2)

    data = {
        "x": a("x"),
        "in_proj_t": a("in_proj_w").T,
        "taps": a("conv_w").T.reshape(NK * DI),
        "norm_w": a("norm_w")[:, None],
        "conv_b": halves(a("conv_b"))[:, :, 0],
        "xproj_t": halves(a("x_proj_w").T),
        "dt_w_t": a("dt_w").T,
        "dt_b": halves(a("dt_b"))[:, :, 0],
        "A_log": halves(a("A_log")),
        "Dp": halves(a("Dp"))[:, :, 0],
        "out_t": halves(a("out_proj_w").T),
        "ff1_t": a("ff_w1").T, "b1": a("ff_b1")[:, None],
        "ff2_t": a("ff_w2").T, "b2": a("ff_b2")[:, None],
        "ln_w": a("ff_ln_w"), "ln_b": a("ff_ln_b"),
        "W_in": b("W_in"), "b_in": b("b_in")[:, None],
        "wb_t": b("W_B").T, "b_B": b("b_B")[:, None], "B_mat": b("B_mat"), "C_mat": b("C_mat"),
        "W_D": b("W_D"), "b_D": b("b_D")[:, None], "W_out": b("W_out"), "b_out": b("b_out")[:, None],
        "W_ig": b("W_ig"), "b_ig": b("b_ig")[:, None], "W_fg": b("W_fg"), "b_fg": b("b_fg")[:, None],
        "gamma": b("gamma"), "beta": b("beta"),
        "wq_t": f("w_q").T.reshape(GR, DK, P).transpose(1, 0, 2),
        "key_t": f("keys").transpose(3, 2, 0, 1).reshape(DK, GR, KEYS),
        "experts": np.concatenate([f("w_down"), f("w_up")], axis=1),
    }
    data = {k: np.ascontiguousarray(v) for k, v in data.items()}

    nc = bacc.Bacc("TRN2", target_bir_lowering=False, num_devices=1)
    tensors = {k: nc.dram_tensor("in_" + k, v.shape, mybir.dt.from_np(v.dtype), kind="ExternalInput").ap()
               for k, v in data.items()}
    tensors["x"] = tensors["x"].rearrange("b (t p) d -> b p t d", p=P)
    y = nc.dram_tensor("y", (NB, T, P), F32, kind="ExternalOutput").ap()
    tensors["y"] = y.rearrange("b (t p) d -> b p t d", p=P)
    build(nc, tensors)
    return run_bass_kernel_spmd(nc, [{"in_" + k: v for k, v in data.items()}], core_ids=[0]).results[0]["y"]
```

```python
from contextlib import ExitStack

import concourse.bass as bass
from concourse import mybir

ALU = mybir.AluOpType
ACT = mybir.ActivationFunctionType
F32 = mybir.dt.float32
BF16 = mybir.dt.bfloat16
I32 = mybir.dt.int32
U32 = mybir.dt.uint32
AX_X = mybir.AxisListType.X

P = 128
NB, T = 16, 512
NT = T // P
DI = 256
NH = DI // P
NS = 16
NK = 4
DR = 8
HEADS, KEYS, DK = 8, 32, 64
GR = 2 * HEADS
SIM = GR * KEYS
EPS = 1e-5
EXP_AND_LN = "natural_log_exp_and_others"
GELU_AND_TANH = "gelu_and_others"
SILU = "silu_and_others"
SIGMOID = "sigmoid_and_others"

BC = 2 * NS
PART = (0, 64, 96)
DT0 = 32
IG, FG, BX = 0, 32, 64

NDA = 4
NBC = 3
NP = 3
NCR = 2
BUFFER = [n % NP for n in range(NS - 1)] + [(NS - 3) % NP]
SPREAD = [(0, 0)] + [x for n in range(NS) for x in ((0, n + 1), (1, n)) if x[1] < NS]
LEAD = 3

PRE, CORE, PA, PB, PC, PD = "pre", "core", "A", "B", "C", "D"
OFFSET = {PRE: 1, CORE: 0, PA: -1, PB: -2, PC: -3, PD: -4}
LAST_ITERATION = NB - 1 + 4
LOOP_FROM, LOOP_TO = 5, 15

SLOTS = {
    "pe_turn_x": (PRE, (2,)), "pe_conv": (PRE, (4, 5, 6, 7)), "pe_xproj": (PRE, (8,)), "pe_dt": (PRE, (9, 10)),
    "pe_skip": (CORE, (5,)),
    "pe_out": (PA, (0,)), "pe_ff1": (PA, (0,)), "pe_ff2": (PA, (2,)),
    "pe_turn_e1": (PA, (6,)), "pe_sim_e1": (PA, (7, 9, 10, 11)), "pe_sum_e1": (PB, (7, 8)),
    "pe_turn_b": (PB, (11,)), "pe_xp": (PB, (12,)), "pe_gate": (PB, (14,)), "pe_y": (PB, (16,)),
    "pe_z": (PC, (3,)),
    "pe_turn_e2": (PC, (12,)), "pe_sim_e2": (PC, (14, 15, 16, 16)), "pe_sum_e2": (PD, (13, 14)),
    "act_rstd_x": (PRE, (1,)), "act_rms_x": (PRE, (2,)), "act_keep_x": (PRE, (3,)), "act_turn_x": (PRE, (4,)),
    "act_conv": (PRE, (5, 6, 7, 8)), "act_silu": (PRE, (8,)), "act_dbl": (PRE, (9,)), "act_soft": (PRE, (10, 12)),
    "act_split": (PRE, (10, 11)), "act_exp": (PRE, (12,)), "act_ln": (PRE, (12,)),
    "act_skip": (CORE, (2,)),
    "act_out": (PA, (1,)), "act_gelu": (PA, (2,)), "act_rstd_a": (PA, (4,)), "act_norm_a": (PA, (5,)),
    "act_rstd_e1": (PA, (6,)), "act_turn_e1": (PA, (7,)), "act_gelu_e1": (PB, (5,)),
    "act_scale_e1": (PB, (5, 5, 6, 7)), "act_out_e1": (PB, (10,)),
    "act_rstd_b": (PB, (11,)), "act_turn_b": (PB, (12,)), "act_xp": (PB, (14,)), "act_gate": (PB, (15,)),
    "act_tanh": (PC, (2,)), "act_rstd_c": (PC, (5,)), "act_norm_c": (PC, (6,)),
    "act_rstd_e2": (PC, (11,)), "act_turn_e2": (PC, (14,)), "act_gelu_e2": (PD, (8,)),
    "act_scale_e2": (PD, (11, 11, 12, 12)), "act_out_e2": (PD, (15,)),
    "dve_stats_x": (PRE, (0,)), "dve_square_x": (PRE, (1,)), "dve_norm_x": (PRE, (2,)),
    "dve_stats_a": (PA, (3,)), "dve_offset_a": (PA, (4,)), "dve_stats_e1": (PA, (5,)), "dve_norm_e1": (PA, (6,)),
    "dve_top_e1": (PA, (9, 10, 11, 12)), "dve_index_e1": (PA, (13,)), "dve_dot_e1": (PB, (0, 1, 1, 4)),
    "dve_weigh_e1": (PB, (4,)), "dve_stats_b": (PB, (10,)), "dve_norm_b": (PB, (11,)), "dve_scan_b": (PB, (15,)),
    "dve_stats_c": (PC, (4,)), "dve_offset_c": (PC, (5,)), "dve_stats_e2": (PC, (9,)), "dve_norm_e2": (PC, (12,)),
    "dve_top_e2": (PC, (15, 16, 16, 17)), "dve_index_e2": (PC, (17,)), "dve_dot_e2": (PD, (5, 7, 7, 8)),
    "dve_weigh_e2": (PD, (9,)),
    "pool_rest": (PRE, (10,)), "pool_delta": (PRE, (12,)), "pool_x1": (PA, (3,)), "pool_x3": (PC, (7,)),
    "pool_fetch_e1": (PA, (12, 13, 14, 15)), "pool_fetch_e2": (PD, (1, 2, 5, 5)),
}

POOL_STATES = (1, 9, 11,)
DVE_STATES = tuple(n for n in range(NS) if n not in POOL_STATES)


def shift(stage, k):
    phase, slots = SLOTS[stage]
    return OFFSET[phase] - slots[k] // NS


def due(stage, i, q, n):
    for k, slot in enumerate(SLOTS[stage][1]):
        o = shift(stage, k)
        assert min(OFFSET.values()) <= o <= max(OFFSET.values())
        if slot % NS == n and (not isinstance(i, int) or 0 <= i + o < NB):
            yield i + o, (q + o) % 2, k


def at(b, per, k=0):
    return b * per + (k + 1)


def later(b):
    return not (isinstance(b, int) and b == 0)


def second(b):
    return not (isinstance(b, int) and b < 2)


def phases(i):
    return {p for p, o in OFFSET.items() if 0 <= i + o < NB}


def run_pipeline(eng, iteration):
    iteration(-1, 1, phases(-1))
    for i in range(LOOP_FROM):
        iteration(i, i % 2, phases(i))
    every = set(OFFSET)
    with eng.Fori(LOOP_FROM, LOOP_TO - 1, 2) as i:
        iteration(i, LOOP_FROM % 2, every)
        iteration(i + 1, 1 - LOOP_FROM % 2, every)
    for i in range(LOOP_TO, LAST_ITERATION + 1):
        iteration(i, i % 2, phases(i))


def build(nc, A):
    with ExitStack() as ctx:
        def sb(name, shape, dt=F32):
            return ctx.enter_context(nc.sbuf_tensor(name, shape, dt))

        def sem(name):
            return ctx.enter_context(nc.semaphore(name))

        ident = sb("ident", [P, P])
        pick = sb("pick", [P, BC], BF16)
        w_taps = sb("w_taps", [P, NK, DI])
        w_res = sb("w_res", [P, DI])
        w_xproj = sb("w_xproj", [P, NH, P])
        w_dt = sb("w_dt", [P, DI])
        w_out = sb("w_out", [P, NH, P])
        w_ff1 = sb("w_ff1", [P, P])
        w_ff2 = sb("w_ff2", [P, P])
        w_xp = sb("w_xp", [P, P])
        w_gate = sb("w_gate", [P, P])
        w_c = sb("w_c", [P, P])
        w_d = sb("w_d", [P, P])
        w_y = sb("w_y", [P, P])
        w_sim = sb("w_sim", [P, SIM])
        ln_w = sb("ln_w", [P, P])
        ln_b = sb("ln_b", [P, P])
        gamma = sb("gamma", [P, P])
        beta = sb("beta", [P, P])
        rank_rev = sb("rank_rev", [P, SIM], BF16)
        decay = sb("decay", [P, NH, NS])
        norm_w = sb("norm_w", [P, 1])
        conv_b = sb("conv_b", [P, NH])
        dt_b = sb("dt_b", [P, NH])
        d_skip = sb("d_skip", [P, NH])
        b_ff1 = sb("b_ff1", [P, 1])
        b_ff2 = sb("b_ff2", [P, 1])
        b_xp = sb("b_xp", [P, 1])
        b_y = sb("b_y", [P, 1])
        b_xpy = sb("b_xpy", [P, 1])
        b_d = sb("b_d", [P, 1])
        b_gate = sb("b_gate", [P, 1])
        b_wb = sb("b_wb", [P, 1])
        b_bx = sb("b_bx", [P, 1])
        b_mat = sb("b_mat", [P, NS])
        eps = sb("eps", [P, 1])
        idle_dve = sb("idle_dve", [P, 1])
        mask = sb("mask", [P, NT, SIM], BF16)

        x_in = sb("x_in", [P, NT, P])
        xn0 = [sb(f"xn0_{q}", [P, NT, P]) for q in range(2)]
        xr = sb("xr", [P, NT, P])
        xrT = sb("xrT", [P, NK - 1 + T])
        ucs = [sb(f"ucs{q}", [P, 2 * NH, T]) for q in range(2)]
        dbl = sb("dbl", [P, T])
        split = [sb(f"split{q}", [P, T], BF16) for q in range(2)]
        soft = sb("soft", [P, NH, T])
        delta = [sb(f"delta{q}", [P, NH, T]) for q in range(2)]
        du = [sb(f"du{q}", [P, NH, T]) for q in range(2)]
        st0, mv0 = sb("st0", [P, NT, 6]), sb("mv0", [P, NT, 2])
        ln0, rs0, m20, rr0, s20 = (sb(n, [P, NT]) for n in ("ln0", "rs0", "m20", "rr0", "s20"))

        dA = sb("dA", [P, NDA, NH, T])
        hp = sb("hp", [P, NP, NH, T])
        c_row = sb("c_row", [P, NCR, T])

        outT, outTb, h1T, x_res = (sb(n, [P, T]) for n in ("outT", "outTb", "h1T", "x_res"))
        rest = h1T
        stA, mvA, lnA, rsA = sb("stA", [P, NT, 6]), sb("mvA", [P, NT, 2]), sb("lnA", [P, NT]), sb("rsA", [P, NT])
        stB, mvB, lnB, rsB = sb("stB", [P, NT, 6]), sb("mvB", [P, NT, 2]), sb("lnB", [P, NT]), sb("rsB", [P, NT])
        stC, mvC, lnC, rsC = sb("stC", [P, NT, 6]), sb("mvC", [P, NT, 2]), sb("lnC", [P, NT]), sb("rsC", [P, NT])
        x1 = [sb(f"x1_{q}", [P, NT, P]) for q in range(2)]
        x2 = sb("x2", [P, NT, P])
        x3 = [sb(f"x3_{q}", [P, NT, P]) for q in range(2)]
        xnb = sb("xnb", [P, NT, P])
        xnbT = sb("xnbT", [P, T])
        xpT, xpTb, gates = (sb(n, [P, T]) for n in ("xpT", "xpTb", "gates"))
        offA, offC, off0 = (sb(n, [P, NT]) for n in ("offA", "offC", "off0"))

        class Experts:

            def __init__(self, n):
                self.xn = sb(f"xn{n}", [P, NT, P])
                self.xnT = sb(f"xnT{n}", [P, T])
                self.rows = sb(f"rows{n}", [P, NT, HEADS, 2 * P])
                self.st, self.mv = sb(f"st{n}", [P, NT, 6]), sb(f"mv{n}", [P, NT, 2])
                self.ln, self.rs = sb(f"ln{n}", [P, NT]), sb(f"rs{n}", [P, NT])
                self.top = sb(f"top{n}", [P, NT, GR])
                self.rank = sb(f"rank{n}", [P, NT, GR])
                self.code = sb(f"code{n}", [P, NT, HEADS])
                self.score = sb(f"score{n}", [P, NT, HEADS])
                self.index = sb(f"index{n}", [P, NT, HEADS], U32)
                self.dot = sb(f"dot{n}", [P, NT, HEADS])
                self.act = sb(f"act{n}", [P, NT, HEADS])
                self.coef = sb(f"coef{n}", [P, NT, HEADS])
                self.mark = sb(f"mark{n}", [P, 1])
                self.started = sem(f"e{n}_started")
                self.stats = sem(f"e{n}_stats")
                self.logged = sem(f"e{n}_logged")
                self.rstd = sem(f"e{n}_rstd")
                self.normed = sem(f"e{n}_normed")
                self.turned = sem(f"e{n}_turned")
                self.turned_sb = sem(f"e{n}_turned_sb")
                self.sim = sem(f"e{n}_sim")
                self.topped = sem(f"e{n}_topped")
                self.masked = sem(f"e{n}_masked")
                self.picks = sem(f"e{n}_picks")
                self.indexed = sem(f"e{n}_indexed")
                self.fetched = [sem(f"e{n}_fetched{t}") for t in range(NT)]
                self.dotted = sem(f"e{n}_dotted")
                self.gelu = sem(f"e{n}_gelu")
                self.weighed = sem(f"e{n}_weighed")
                self.scaled = sem(f"e{n}_scaled")
                self.summed = sem(f"e{n}_summed")
                self.added = sem(f"e{n}_added")

        e1, e2 = Experts(1), Experts(2)

        bcast = [ctx.enter_context(nc.psum_tensor(f"bcast{k}", [P, 1, T], F32)) for k in range(NBC)]
        ysum = ctx.enter_context(nc.psum_tensor("ysum", [P, NH, T], F32))
        bank = [ctx.enter_context(nc.psum_tensor(f"bank{k}", [P, T], F32)) for k in range(3)]

        weights_in = sem("weights_in")
        cleared = sem("cleared")
        made = sem("made")
        folded = sem("folded")
        x_loaded = sem("x_loaded")
        p_stats = sem("p_stats")
        p_logged = sem("p_logged")
        p_rstd = sem("p_rstd")
        p_square = sem("p_square")
        p_scale = sem("p_scale")
        p_offset = sem("p_offset")
        p_kept = sem("p_kept")
        p_normed = sem("p_normed")
        p_turned = sem("p_turned")
        p_turned_sb = sem("p_turned_sb")
        conv_mm = sem("conv_mm")
        conv_sb = sem("conv_sb")
        silu_done = sem("silu_done")
        dbl_mm = sem("dbl_mm")
        dbl_sb = sem("dbl_sb")
        rest1 = sem("rest1")
        part2 = sem("part2")
        rest2 = sem("rest2")
        split_done = sem("split_done")
        dt_mm = sem("dt_mm")
        dt_sb = sem("dt_sb")
        dt_exp = sem("dt_exp")
        dt_log = sem("dt_log")
        delta_done = sem("delta_done")
        du_done = sem("du_done")
        decays = sem("decays")
        b_spread = sem("b_spread")
        c_spread = sem("c_spread")
        fed = sem("fed")
        scanned = sem("scanned")
        read_out = sem("read_out")
        c_kept = sem("c_kept")
        pool_read = sem("pool_read")
        y_sum = sem("y_sum")
        skip_scaled = sem("skip_scaled")
        y_gated = sem("y_gated")
        xres_loaded = sem("xres_loaded")
        a_out = sem("a_out")
        a_out_sb = sem("a_out_sb")
        a_h1 = sem("a_h1")
        a_h1_sb = sem("a_h1_sb")
        a_z = sem("a_z")
        a_stats = sem("a_stats")
        a_logged = sem("a_logged")
        a_rstd = sem("a_rstd")
        a_offset = sem("a_offset")
        a_normed = sem("a_normed")
        a_affine = sem("a_affine")
        x1_done = sem("x1_done")
        b_stats = sem("b_stats")
        b_logged = sem("b_logged")
        b_rstd = sem("b_rstd")
        b_normed = sem("b_normed")
        c_stats = sem("c_stats")
        c_logged = sem("c_logged")
        c_rstd = sem("c_rstd")
        c_offset = sem("c_offset")
        c_normed = sem("c_normed")
        b_turned = sem("b_turned")
        b_turned_sb = sem("b_turned_sb")
        b_xp_mm = sem("b_xp_mm")
        b_xp_sb = sem("b_xp_sb")
        b_gate_mm = sem("b_gate_mm")
        b_gate_sb = sem("b_gate_sb")
        b_fed = sem("b_fed")
        b_scanned = sem("b_scanned")
        b_y_mm = sem("b_y_mm")
        b_y_sb = sem("b_y_sb")
        b_z = sem("b_z")
        b_affine = sem("b_affine")
        x3_done = sem("x3_done")
        stored = sem("stored")

        tmp1 = e1.rows[:, 0, :, :].rearrange("p a b -> p (a b)")
        tmp2 = e1.rows[:, 1, :, :].rearrange("p a b -> p (a b)")
        tmp3 = e1.rows[:, 2, :, :].rearrange("p a b -> p (a b)")
        wq_t = tmp1[0:DK, 0:GR * P].rearrange("c (g d) -> c g d", g=GR)
        key_t = tmp2[0:DK, 0:SIM].rearrange("c (g k) -> c g k", g=GR)
        in_t = tmp2[:, 512:1024]
        wb_t = tmp2[:, 1024:1024 + P]
        taps = tmp3[:, 0:NK * DI].rearrange("p (k d) -> p k d", k=NK)
        rank_i = e1.rows[:, 3, 0:2, :].rearrange("p a b -> p (a b)").bitcast(I32)

        def everywhere(row):
            return row.partition_broadcast(P)

        loads = [
            (in_t, A["in_proj_t"]), (wq_t, A["wq_t"]), (key_t, A["key_t"]), (wb_t, A["wb_t"]),
            (taps.rearrange("p k d -> p (k d)"), everywhere(A["taps"])),
            (ln_w[:], everywhere(A["ln_w"])), (ln_b[:], everywhere(A["ln_b"])),
            (gamma[:], everywhere(A["gamma"])), (beta[:], everywhere(A["beta"])),
            (w_dt[DT0:DT0 + DR, :], A["dt_w_t"]), (w_out[:], A["out_t"]), (w_ff1[:], A["ff1_t"]),
            (w_ff2[:], A["ff2_t"]), (w_xp[:], A["W_in"]), (w_gate[:, IG:IG + NS], A["W_ig"]),
            (w_gate[:, FG:FG + NS], A["W_fg"]), (w_c[IG:IG + NS, :], A["C_mat"]), (w_d[:], A["W_D"]),
            (w_y[:], A["W_out"]), (decay[:], A["A_log"]), (norm_w[:], A["norm_w"]),
            (conv_b[:], A["conv_b"]), (dt_b[:], A["dt_b"]), (d_skip[:], A["Dp"]), (b_ff1[:], A["b1"]),
            (b_ff2[:], A["b2"]), (b_xp[:], A["b_in"]), (b_y[:], A["b_out"]), (b_d[:], A["b_D"]),
            (b_gate[IG:IG + NS, :], A["b_ig"]), (b_gate[FG:FG + NS, :], A["b_fg"]),
            (b_wb[:], A["b_B"]), (b_mat[:], A["B_mat"]),
            (w_xproj[:, :, DT0:DT0 + DR], A["xproj_t"][:, :, 0:DR]),
        ] + [(w_xproj[:, :, r:r + BC], A["xproj_t"][:, :, DR:DR + BC]) for r in PART]

        with nc.Block() as setup:
            @setup.sync
            def _(sp):
                sp.wait_ge(cleared, 1)
                for dst, src in loads:
                    sp.dma_start(dst, src).then_inc(weights_in, 16)

            @setup.gpsimd
            def _(pool):
                pool.memset(ident[:], 0.0).then_inc(made, 1)
                pool.wait_ge(made, 1)
                pool.affine_select(out=ident[:], in_=ident[:], compare_op=ALU.not_equal, fill=1.0, base=0,
                                   pattern=[[-1, P]], channel_multiplier=1).then_inc(made, 1)
                pool.iota(rank_i, pattern=[[0, GR], [-1, KEYS]], base=KEYS, channel_multiplier=0).then_inc(made, 1)

            @setup.vector
            def _(dve):
                for tile in (w_xproj, w_dt, w_gate, w_c, b_gate, gates, dA, xrT, split[0], split[1], dbl):
                    nc.vector.memset(tile[:], 0.0)
                nc.vector.memset(eps[:], EPS).then_inc(cleared, 1)
                dve.wait_ge(made, 3)
                nc.vector.tensor_copy(rank_rev[:], rank_i)
                dve.wait_ge(cleared, 1)
                nc.vector.tensor_tensor(pick[:], ident[:, 0:BC], ident[:, PART[1]:PART[1] + BC],
                                        ALU.add).then_inc(cleared, 1)
                dve.wait_ge(cleared, 2)
                nc.vector.tensor_tensor(pick[:], pick[:], ident[:, PART[2]:PART[2] + BC], ALU.add)
                dve.wait_ge(weights_in, 16 * len(loads))
                nc.vector.tensor_scalar(in_t, in_t, norm_w[:, 0:1], None, ALU.mult).then_inc(cleared, 1)
                dve.wait_ge(cleared, 3)
                nc.vector.tensor_copy(w_res[:], in_t[:, DI:2 * DI])
                for k in range(NK):
                    nc.vector.tensor_tensor(w_taps[:, k, :], in_t[:, 0:DI], taps[:, k, :], ALU.mult)
                nc.vector.tensor_tensor(b_xpy[:], b_xp[:], b_y[:], ALU.add)
                dve.wait_ge(folded, 1)
                nc.vector.tensor_copy(w_sim[:], bank[0][:])
                nc.vector.tensor_copy(w_gate[:, BX:BX + NS], bank[1][:, 0:NS])
                nc.vector.tensor_copy(b_bx[0:NS, :], bank[1][0:NS, NS:NS + 1]).then_inc(cleared, 1)

            @setup.scalar
            def _(act):
                act.wait_ge(weights_in, 16 * len(loads))
                nc.scalar.activation(decay[:], decay[:], ACT.Exp).then_inc(p_scale, 1)
                act.wait_ge(p_scale, 1)
                nc.scalar.mul(decay[:], decay[:], -1.0).then_inc(p_scale, 1)

            @setup.tensor
            def _(pe):
                pe.wait_ge(weights_in, 16 * len(loads))
                for g in range(GR):
                    nc.tensor.matmul(bank[0][:, g * KEYS:(g + 1) * KEYS], wq_t[:, g, :], key_t[:, g, :],
                                     start=True, stop=True, skip_group_check=True)
                nc.tensor.matmul(bank[1][:, 0:NS], wb_t, b_mat[:], start=True, stop=True, skip_group_check=True)
                nc.tensor.matmul(bank[1][0:NS, NS:NS + 1], b_mat[:], b_wb[:], start=True, stop=True,
                                 skip_group_check=True).then_inc(folded, 1)

        P_SCALE0 = 2

        def multiplied(c, n):
            if n in POOL_STATES:
                return pool_read, at(c, len(POOL_STATES), POOL_STATES.index(n))
            return read_out, at(c, len(DVE_STATES), DVE_STATES.index(n))

        def spread_used(c, k):
            w, n = SPREAD[k]
            if w == 0:
                return fed, at(c, NS, n)
            if n in POOL_STATES:
                return c_kept, at(c, len(POOL_STATES), POOL_STATES.index(n))
            return multiplied(c, n)

        block = ctx.enter_context(nc.Block())

        @block.sync
        def _(sp):
            def iteration(i, q, has):
                b = {p: i + o for p, o in OFFSET.items()}
                if PRE in has:
                    n = b[PRE]
                    if later(n):
                        sp.wait_ge(p_normed, at(n - 1, 1))
                        sp.wait_ge(p_kept, at(n - 1, 1))
                    sp.dma_start(x_in[:], A["x"][n]).then_inc(x_loaded, 16)
                if PA in has:
                    n = b[PA]
                    if later(n):
                        sp.wait_ge(x1_done, at(n - 1, 1))
                    sp.dma_start(x_res[:].rearrange("p (a d) -> p a d", a=NT), A["x"][n]).then_inc(xres_loaded, 16)
                if PD in has:
                    n = b[PD]
                    sp.wait_ge(e2.added, at(n, 1))
                    sp.dma_start(A["y"][n], x3[q][:]).then_inc(stored, 16)

            run_pipeline(sp, iteration)
            sp.wait_ge(stored, 16 * NB)

        @block.tensor
        def _(pe):
            busy, half_done = {}, set()

            def claim(k, i):
                assert k not in half_done
                if k in busy:
                    s, per, nth, off = busy[k]
                    pe.wait_ge(s, at(i + off, per, nth))

            def fill(k, stage, step, s, per, nth=0):
                busy[k] = (s, per, nth, shift(stage, step))

            def turn(k, src, s):
                for t in range(NT):
                    mm = nc.tensor.transpose(bank[k][:, t * P:(t + 1) * P], src[:, t, :], ident[:])
                mm.then_inc(s, 1)

            def experts_sim(e, k, i, m, stage, t):
                claim(k, i)
                if t == 0:
                    pe.wait_ge(e.turned_sb, at(m, 1))
                nc.tensor.matmul(bank[k][:], e.xnT[:, t * P:(t + 1) * P], w_sim[:], start=True,
                                 stop=True).then_inc(e.sim, 1)
                fill(k, stage, t, e.masked, NT, t)

            def experts_sum(e, k, i, m, stage, half, residual):
                if half == 0:
                    claim(k, i)
                    half_done.add(k)
                    nc.tensor.matmul(bank[k][:].rearrange("p (t d) -> p t d", t=NT), ident[:], residual[:],
                                     start=True, stop=False)
                    pe.wait_ge(e.scaled, at(m, NT, NT - 1))
                for h in range(half * HEADS // 2, (half + 1) * HEADS // 2):
                    mm = nc.tensor.matmul(bank[k][:].rearrange("p (t d) -> p t d", t=NT), ident[:],
                                          e.rows[:, :, h, P:2 * P], start=False, stop=(h == HEADS - 1))
                if half == 1:
                    half_done.remove(k)
                    mm.then_inc(e.summed, 1)
                    fill(k, stage, half, e.added, 1)

            def iteration(i, q, has):
                for k in busy:
                    s, per, nth, off = busy[k]
                    busy[k] = (s, per, nth, off - 1)
                b = {p: i + o for p, o in OFFSET.items()}

                def spread(c, part, k):
                    w, n = SPREAD[k]
                    if k == 0:
                        pe.wait_ge(split_done, at(c, 1))
                    if k >= NBC:
                        pe.wait_ge(*spread_used(c, k - NBC))
                    elif later(c):
                        pe.wait_ge(*spread_used(c - 1, max(x for x in range(2 * NS) if x % NBC == k)))
                    r = w * NS + n
                    nc.tensor.matmul(bcast[k % NBC][:, 0, :], pick[:, r:r + 1].to_broadcast([P, P]), part[:],
                                     start=True, stop=True).then_inc((b_spread, c_spread)[w], 1)

                for n in range(NS):
                    if PRE in has and n == NS - 1:
                        spread(b[PRE], split[1 - q], 0)
                    if CORE in has:
                        c = b[CORE]
                        for k in range(2 * n + 3, min(2 * n + 5, 2 * NS)):
                            spread(c, split[q], k)
                        if n == 1 and later(c):
                            pe.wait_ge(y_gated, at(c - 1, 1))
                        for k in [n - 1] * (n > 0) + [n] * (n == NS - 1):
                            pe.wait_ge(*multiplied(c, k))
                            for j in range(NH):
                                mm = nc.tensor.matmul(ysum[:, j, :], ident[:], hp[:, BUFFER[k], j, :],
                                                      start=(k == 0), stop=(k == NS - 1))
                            mm.then_inc(y_sum, 1)
                    for m, r, _ in due("pe_skip", i, q, n):
                        pe.wait_ge(skip_scaled, at(m, 1))
                        for j in range(NH):
                            nc.tensor.matmul(ysum[:, j, :], ident[:], ucs[r][:, j, :], start=False, stop=False)
                    for m, r, k in due("pe_sim_e2", i, q, n):
                        experts_sim(e2, 0, i, m, "pe_sim_e2", k)
                    for m, r, _ in due("pe_turn_x", i, q, n):
                        claim(0, i)
                        pe.wait_ge(p_normed, at(m, 1))
                        turn(0, xr, p_turned)
                        fill(0, "pe_turn_x", 0, p_turned_sb, 1)
                    for m, r, k in due("pe_conv", i, q, n):
                        claim(0, i)
                        if k == 0:
                            pe.wait_ge(p_turned_sb, at(m, 1))
                        if k < NH:
                            for tap in range(NK):
                                mm = nc.tensor.matmul(bank[0][:], w_taps[:, tap, k * P:(k + 1) * P],
                                                      xrT[:, tap:tap + T], start=(tap == 0), stop=(tap == NK - 1))
                        else:
                            mm = nc.tensor.matmul(bank[0][:], w_res[:, (k - NH) * P:(k - NH + 1) * P],
                                                  xrT[:, NK - 1:NK - 1 + T], start=True, stop=True)
                        mm.then_inc(conv_mm, 1)
                        fill(0, "pe_conv", k, conv_sb, 2 * NH, k)
                    for m, r, _ in due("pe_xproj", i, q, n):
                        claim(0, i)
                        pe.wait_ge(silu_done, at(m, 1))
                        for j in range(NH):
                            mm = nc.tensor.matmul(bank[0][:], w_xproj[:, j, :], ucs[r][:, j, :],
                                                  start=(j == 0), stop=(j == NH - 1))
                        mm.then_inc(dbl_mm, 1)
                        fill(0, "pe_xproj", 0, dbl_sb, 1)
                    for m, r, k in due("pe_dt", i, q, n):
                        claim(0, i)
                        if k == 0:
                            pe.wait_ge(dbl_sb, at(m, 1))
                        nc.tensor.matmul(bank[0][:], w_dt[:, k * P:(k + 1) * P], dbl[:], start=True,
                                         stop=True).then_inc(dt_mm, 1)
                        fill(0, "pe_dt", k, dt_sb, NH, k)
                    for m, r, _ in due("pe_turn_e2", i, q, n):
                        claim(0, i)
                        pe.wait_ge(e2.normed, at(m, 1))
                        turn(0, e2.xn, e2.turned)
                        fill(0, "pe_turn_e2", 0, e2.turned_sb, 1)
                    if PRE in has and n == NS - 1:
                        for k in range(1, NBC):
                            spread(b[PRE], split[1 - q], k)
                    for m, r, _ in due("pe_out", i, q, n):
                        claim(1, i)
                        pe.wait_ge(y_gated, at(m, 1))
                        pe.wait_ge(p_kept, at(m, 1))
                        for j in range(NH):
                            nc.tensor.matmul(bank[1][:], w_out[:, j, :], ucs[r][:, j, :], start=(j == 0),
                                             stop=False, skip_group_check=True)
                        for t in range(NT):
                            mm = nc.tensor.matmul(bank[1][:, t * P:(t + 1) * P], xn0[r][:, t, :], ident[:],
                                                  start=False, stop=True, skip_group_check=True)
                        mm.then_inc(a_out, 1)
                        fill(1, "pe_out", 0, a_out_sb, 1)
                    for m, r, _ in due("pe_ff1", i, q, n):
                        claim(1, i)
                        pe.wait_ge(a_out_sb, at(m, 1))
                        nc.tensor.matmul(bank[1][:], w_ff1[:], outT[:], start=True, stop=True).then_inc(a_h1, 1)
                        fill(1, "pe_ff1", 0, a_h1_sb, 1)
                    for m, r, _ in due("pe_ff2", i, q, n):
                        claim(1, i)
                        pe.wait_ge(a_h1_sb, at(m, 1))
                        for t in range(NT):
                            tok = slice(t * P, (t + 1) * P)
                            nc.tensor.matmul(bank[1][:, tok], h1T[:, tok], w_ff2[:], start=True, stop=False,
                                             skip_group_check=True)
                            mm = nc.tensor.matmul(bank[1][:, tok], outTb[:, tok], ident[:], start=False,
                                                  stop=True, skip_group_check=True)
                        mm.then_inc(a_z, 1)
                        fill(1, "pe_ff2", 0, a_normed, 1)
                    for m, r, _ in due("pe_turn_e1", i, q, n):
                        claim(1, i)
                        pe.wait_ge(e1.normed, at(m, 1))
                        turn(1, e1.xn, e1.turned)
                        fill(1, "pe_turn_e1", 0, e1.turned_sb, 1)
                    for m, r, k in due("pe_sim_e1", i, q, n):
                        experts_sim(e1, 1, i, m, "pe_sim_e1", k)
                    for m, r, _ in due("pe_z", i, q, n):
                        claim(2, i)
                        pe.wait_ge(b_y_sb, at(m, 1))
                        for t in range(NT):
                            tok = slice(t * P, (t + 1) * P)
                            nc.tensor.matmul(bank[2][:, tok], xnbT[:, tok], w_y[:], start=True, stop=False,
                                             skip_group_check=True)
                            mm = nc.tensor.matmul(bank[2][:, tok], xpTb[:, tok], ident[:], start=False,
                                                  stop=True, skip_group_check=True)
                        mm.then_inc(b_z, 1)
                        fill(2, "pe_z", 0, c_normed, 1)
                    for m, r, k in due("pe_sum_e1", i, q, n):
                        experts_sum(e1, 2, i, m, "pe_sum_e1", k, x1[r])
                    for m, r, _ in due("pe_turn_b", i, q, n):
                        claim(2, i)
                        pe.wait_ge(b_normed, at(m, 1))
                        turn(2, xnb, b_turned)
                        fill(2, "pe_turn_b", 0, b_turned_sb, 1)
                    for m, r, _ in due("pe_xp", i, q, n):
                        claim(2, i)
                        pe.wait_ge(b_turned_sb, at(m, 1))
                        nc.tensor.matmul(bank[2][:], w_xp[:], xnbT[:], start=True, stop=True).then_inc(b_xp_mm, 1)
                        fill(2, "pe_xp", 0, b_xp_sb, 1)
                    for m, r, _ in due("pe_gate", i, q, n):
                        claim(2, i)
                        pe.wait_ge(b_xp_sb, at(m, 1))
                        nc.tensor.matmul(bank[2][:], w_gate[:], xpT[:], start=True, stop=True).then_inc(b_gate_mm, 1)
                        fill(2, "pe_gate", 0, b_fed, 1)
                    for m, r, _ in due("pe_y", i, q, n):
                        claim(2, i)
                        nc.tensor.matmul(bank[2][:], w_d[:], xpT[:], start=True, stop=False)
                        pe.wait_ge(b_scanned, at(m, 1))
                        nc.tensor.matmul(bank[2][:], w_c[:], gates[:], start=False, stop=True).then_inc(b_y_mm, 1)
                        fill(2, "pe_y", 0, b_y_sb, 1)
                    for m, r, k in due("pe_sum_e2", i, q, n):
                        experts_sum(e2, 1, i, m, "pe_sum_e2", k, x3[r])

            run_pipeline(pe, iteration)

        @block.scalar
        def _(act):
            table = [None]

            def needs(name):
                if table[0] != name:
                    act.preload_act_table_set(name)
                    table[0] = name

            def inverse_root(var, ln, out, logged, ln_at, done):
                nc.scalar.activation(ln[:], var, ACT.Ln, bias=eps[:, 0:1]).then_inc(logged, 1)
                act.wait_ge(logged, ln_at)
                nc.scalar.activation(out[:], ln[:], ACT.Exp, scale=-0.5).then_inc(done, 1)

            def normalise(dst, src, scale, offset, s):
                for t in range(NT):
                    op = nc.scalar.activation(dst[:, t, :], src[:, t, :], ACT.Identity, scale=scale[:, t:t + 1],
                                              bias=offset[:, t:t + 1])
                op.then_inc(s, 1)

            def tokens(k):
                return bank[k][:].rearrange("p (t d) -> p t d", t=NT)

            def experts_rstd(e, m):
                needs(EXP_AND_LN)
                act.wait_ge(e.stats, at(m, 2, 1))
                inverse_root(e.mv[:, :, 1], e.ln, e.rs, e.logged, at(m, 1), e.rstd)

            def experts_turned(e, k, m):
                act.wait_ge(e.turned, at(m, 1))
                nc.scalar.activation(e.xnT[:], bank[k][:], ACT.Copy).then_inc(e.turned_sb, 1)

            def experts_gelu(e, m):
                needs(GELU_AND_TANH)
                act.wait_ge(e.dotted, at(m, NT, NT - 1))
                nc.scalar.activation(e.act[:], e.dot[:], ACT.Gelu).then_inc(e.gelu, 1)

            def experts_out(e, k, dst, m):
                act.wait_ge(e.summed, at(m, 1))
                nc.scalar.activation(dst[:], tokens(k), ACT.Copy).then_inc(e.added, 1)

            def experts_scale(e, m, t):
                if t == 0:
                    act.wait_ge(e.weighed, at(m, 1))
                for h in range(HEADS):
                    row = e.rows[:, t, h, P:2 * P]
                    op = nc.scalar.activation(row, row, ACT.Copy, scale=e.coef[:, t, h:h + 1])
                op.then_inc(e.scaled, 1)

            def iteration(i, q, has):
                b = {p: i + o for p, o in OFFSET.items()}

                def decays_of(n):
                    c = b[CORE]
                    needs(EXP_AND_LN)
                    if n == 0:
                        act.wait_ge(delta_done, at(c, 1))
                    if n >= NDA:
                        act.wait_ge(scanned, at(c, NS, n - NDA))
                    elif later(c):
                        act.wait_ge(scanned, at(c - 1, NS, NS + n - NDA))
                    for j in range(NH):
                        op = nc.scalar.activation(dA[:, n % NDA, j, 1:T], delta[q][:, j, 1:T], ACT.Exp,
                                                  scale=decay[:, j, n:n + 1])
                    op.then_inc(decays, 1)

                for n in range(NS):
                    if CORE in has:
                        for k in range(LEAD + 1) if n == 0 else [n + LEAD] if n + LEAD < NS else []:
                            decays_of(k)
                        if n in POOL_STATES:
                            c, k = b[CORE], POOL_STATES.index(n)
                            act.wait_ge(c_spread, at(c, NS, n))
                            if k >= NCR:
                                act.wait_ge(pool_read, at(c, len(POOL_STATES), k - NCR))
                            elif later(c):
                                act.wait_ge(pool_read, at(c - 1, len(POOL_STATES), len(POOL_STATES) + k - NCR))
                            nc.scalar.activation(c_row[:, k % NCR, :], bcast[SPREAD.index((1, n)) % NBC][:, 0, :],
                                                 ACT.Copy).then_inc(c_kept, 1)
                    for m, r, _ in due("act_rstd_x", i, q, n):
                        needs(EXP_AND_LN)
                        act.wait_ge(p_stats, at(m, 2, 1))
                        inverse_root(mv0[:, :, 1], ln0, rs0, p_logged, at(m, 2, 0), p_rstd)
                    for m, r, _ in due("act_rms_x", i, q, n):
                        needs(EXP_AND_LN)
                        act.wait_ge(p_square, at(m, 2, 1))
                        inverse_root(m20[:], ln0, rr0, p_logged, at(m, 2, 1), p_rstd)
                    for m, r, _ in due("act_out", i, q, n):
                        act.wait_ge(a_out, at(m, 1))
                        if later(m):
                            act.wait_ge(x1_done, at(m - 1, 1))
                        nc.scalar.activation(outT[:], bank[1][:], ACT.Copy)
                        nc.scalar.activation(outTb[:], bank[1][:], ACT.Identity,
                                             bias=b_ff2[:, 0:1]).then_inc(a_out_sb, 1)
                    for m, r, _ in due("act_tanh", i, q, n):
                        needs(GELU_AND_TANH)
                        act.wait_ge(b_y_mm, at(m, 1))
                        nc.scalar.activation(xnbT[:], bank[2][:], ACT.Tanh, bias=b_d[:, 0:1]).then_inc(b_y_sb, 1)
                    for m, r, _ in due("act_gelu_e1", i, q, n):
                        experts_gelu(e1, m)
                    for m, r, _ in due("act_gelu", i, q, n):
                        needs(GELU_AND_TANH)
                        act.wait_ge(a_h1, at(m, 1))
                        act.wait_ge(split_done, at(min(m + 1, NB - 1) if isinstance(m, int) else m + 1, 1))
                        nc.scalar.activation(h1T[:], bank[1][:], ACT.Gelu, bias=b_ff1[:, 0:1]).then_inc(a_h1_sb, 1)
                    for m, r, _ in due("act_skip", i, q, n):
                        act.wait_ge(du_done, at(m, 1))
                        for j in range(NH):
                            op = nc.scalar.activation(ucs[r][:, j, :], ucs[r][:, j, :], ACT.Copy,
                                                      scale=d_skip[:, j:j + 1])
                        op.then_inc(skip_scaled, 1)
                    for m, r, _ in due("act_keep_x", i, q, n):
                        act.wait_ge(p_offset, at(m, 1))
                        if second(m):
                            act.wait_ge(a_out, at(m - 2, 1))
                        normalise(xn0[r], x_in, rs0, off0, p_kept)
                    for m, r, _ in due("act_rstd_a", i, q, n):
                        needs(EXP_AND_LN)
                        act.wait_ge(a_stats, at(m, 2, 1))
                        inverse_root(mvA[:, :, 1], lnA, rsA, a_logged, at(m, 1), a_rstd)
                    for m, r, _ in due("act_rstd_c", i, q, n):
                        needs(EXP_AND_LN)
                        act.wait_ge(c_stats, at(m, 2, 1))
                        inverse_root(mvC[:, :, 1], lnC, rsC, c_logged, at(m, 1), c_rstd)
                    for m, r, _ in due("act_norm_a", i, q, n):
                        act.wait_ge(a_offset, at(m, 1))
                        normalise(outT[:].rearrange("p (t d) -> p t d", t=NT), tokens(1), rsA, offA, a_normed)
                    for m, r, _ in due("act_norm_c", i, q, n):
                        act.wait_ge(c_offset, at(m, 1))
                        normalise(xnb, tokens(2), rsC, offC, c_normed)
                    for m, r, _ in due("act_rstd_e1", i, q, n):
                        experts_rstd(e1, m)
                    for m, r, _ in due("act_turn_e1", i, q, n):
                        experts_turned(e1, 1, m)
                    for m, r, _ in due("act_turn_x", i, q, n):
                        act.wait_ge(p_turned, at(m, 1))
                        nc.scalar.activation(xrT[:, NK - 1:NK - 1 + T], bank[0][:], ACT.Copy).then_inc(p_turned_sb, 1)
                    for m, r, k in due("act_conv", i, q, n):
                        act.wait_ge(conv_mm, at(m, 2 * NH, k))
                        if k == 0 and second(m):
                            act.wait_ge(a_out, at(m - 2, 1))
                        if k < NH:
                            op = nc.scalar.activation(ucs[r][:, k, :], bank[0][:], ACT.Identity,
                                                      bias=conv_b[:, k:k + 1])
                        else:
                            op = nc.scalar.activation(ucs[r][:, k, :], bank[0][:], ACT.Copy)
                        op.then_inc(conv_sb, 1)
                    for m, r, _ in due("act_silu", i, q, n):
                        needs(SILU)
                        act.wait_ge(conv_sb, at(m, 2 * NH, 2 * NH - 1))
                        nc.scalar.activation(ucs[r][:], ucs[r][:], ACT.Silu).then_inc(silu_done, 1)
                    for m, r, _ in due("act_dbl", i, q, n):
                        act.wait_ge(dbl_mm, at(m, 1))
                        nc.scalar.activation(dbl[:], bank[0][:], ACT.Copy)
                        nc.scalar.activation(split[r][:], bank[0][:], ACT.Copy).then_inc(dbl_sb, 1)
                    for m, r, k in due("act_soft", i, q, n):
                        act.wait_ge(dt_mm, at(m, NH, k))
                        if k == 0 and later(m):
                            act.wait_ge(delta_done, at(m - 1, 1))
                        nc.scalar.activation(soft[:, k, :], bank[0][:], ACT.Abs, bias=dt_b[:, k:k + 1])
                        nc.scalar.activation(delta[r][:, k, :], bank[0][:], ACT.Relu,
                                             bias=dt_b[:, k:k + 1]).then_inc(dt_sb, 1)
                    for m, r, k in due("act_split", i, q, n):
                        act.wait_ge((rest1, rest2)[k], at(m, 1))
                        nc.scalar.activation(split[r][PART[k + 1]:, :], rest[PART[k + 1]:, :],
                                             ACT.Copy).then_inc((part2, split_done)[k], 1)
                    for m, r, _ in due("act_exp", i, q, n):
                        needs(EXP_AND_LN)
                        act.wait_ge(dt_sb, at(m, NH, NH - 1))
                        nc.scalar.activation(soft[:], soft[:], ACT.Exp, scale=-1.0).then_inc(dt_exp, 1)
                    for m, r, _ in due("act_ln", i, q, n):
                        needs(EXP_AND_LN)
                        act.wait_ge(dt_exp, at(m, 1))
                        nc.scalar.activation(soft[:], soft[:], ACT.Ln, bias=1.0).then_inc(dt_log, 1)
                    for m, r, t in due("act_scale_e1", i, q, n):
                        experts_scale(e1, m, t)
                    for m, r, _ in due("act_out_e1", i, q, n):
                        if later(m):
                            act.wait_ge(x3_done, at(m - 1, 1))
                        experts_out(e1, 2, x2, m)
                    for m, r, _ in due("act_rstd_b", i, q, n):
                        needs(EXP_AND_LN)
                        act.wait_ge(b_stats, at(m, 2, 1))
                        inverse_root(mvB[:, :, 1], lnB, rsB, b_logged, at(m, 1), b_rstd)
                    for m, r, _ in due("act_turn_b", i, q, n):
                        act.wait_ge(b_turned, at(m, 1))
                        nc.scalar.activation(xnbT[:], bank[2][:], ACT.Copy).then_inc(b_turned_sb, 1)
                    for m, r, _ in due("act_xp", i, q, n):
                        act.wait_ge(b_xp_mm, at(m, 1))
                        nc.scalar.activation(xpT[:], bank[2][:], ACT.Identity, bias=b_xp[:, 0:1])
                        nc.scalar.activation(xpTb[:], bank[2][:], ACT.Identity,
                                             bias=b_xpy[:, 0:1]).then_inc(b_xp_sb, 1)
                    for m, r, _ in due("act_gate", i, q, n):
                        needs(SIGMOID)
                        act.wait_ge(b_gate_mm, at(m, 1))
                        nc.scalar.activation(gates[0:FG + NS, :], bank[2][0:FG + NS, :], ACT.Sigmoid,
                                             bias=b_gate[0:FG + NS, 0:1]).then_inc(b_gate_sb, 1)
                    for m, r, _ in due("act_rstd_e2", i, q, n):
                        experts_rstd(e2, m)
                    for m, r, _ in due("act_turn_e2", i, q, n):
                        experts_turned(e2, 0, m)
                    for m, r, _ in due("act_gelu_e2", i, q, n):
                        experts_gelu(e2, m)
                    for m, r, t in due("act_scale_e2", i, q, n):
                        experts_scale(e2, m, t)
                    for m, r, _ in due("act_out_e2", i, q, n):
                        experts_out(e2, 1, x3[r], m)
                needs(EXP_AND_LN)

            run_pipeline(act, iteration)

        @block.vector
        def _(dve):
            def statistics(src, st, mv, s, base):
                for t in range(NT):
                    op = nc.vector.bn_stats(st[:, t, :], src[:, t, :])
                op.then_inc(s, 1)
                dve.wait_ge(s, base)
                nc.vector.memset(idle_dve[:], 0.0)
                for t in range(NT):
                    op = nc.vector.bn_aggr(mv[:, t, :], st[:, t, :])
                op.then_inc(s, 1)

            def tokens(k):
                return bank[k][:].rearrange("p (t d) -> p t d", t=NT)

            def negative_mean(out, mv, scale, s):
                nc.vector.scalar_tensor_tensor(out=out[:], in0=mv[:, :, 0], scalar=-1.0, in1=scale[:],
                                               op0=ALU.mult, op1=ALU.mult).then_inc(s, 1)

            def normalise(dst, src, mv, scale, s):
                for t in range(NT):
                    op = nc.vector.tensor_scalar(dst[:, t, :], src[:, t, :], mv[:, t, 0:1], scale[:, t:t + 1],
                                                 ALU.subtract, ALU.mult)
                op.then_inc(s, 1)

            def experts_top(e, k, n, t):
                dve.wait_ge(e.sim, at(n, NT, t))
                sims = bank[k][:].rearrange("p (g k) -> p g k", g=GR)
                nc.vector.tensor_reduce(e.top[:, t, :], sims, AX_X, ALU.max).then_inc(e.topped, 1)
                dve.wait_ge(e.topped, at(n, NT, t))
                nc.vector.tensor_tensor(mask[:, t, :].rearrange("p (g k) -> p g k", g=GR), sims,
                                        e.top[:, t, :].unsqueeze(2).to_broadcast([P, GR, KEYS]),
                                        ALU.is_equal).then_inc(e.masked, 1)

            def experts_index(e, n):
                dve.wait_ge(e.masked, at(n, NT, NT - 1))
                nc.vector.tensor_tensor(mask[:], mask[:], rank_rev[:].unsqueeze(1).to_broadcast([P, NT, SIM]),
                                        ALU.mult).then_inc(e.picks, 1)
                dve.wait_ge(e.picks, at(n, 3, 0))
                nc.vector.tensor_reduce(e.rank[:], mask[:].rearrange("p t (g k) -> p t g k", g=GR), AX_X,
                                        ALU.max).then_inc(e.picks, 1)
                dve.wait_ge(e.picks, at(n, 3, 1))
                nc.vector.scalar_tensor_tensor(out=e.code[:], in0=e.rank[:, :, 0:HEADS], scalar=-float(KEYS),
                                               in1=e.rank[:, :, HEADS:GR], op0=ALU.mult,
                                               op1=ALU.subtract).then_inc(e.picks, 1)
                dve.wait_ge(e.picks, at(n, 3, 2))
                nc.vector.tensor_tensor(e.score[:], e.top[:, :, 0:HEADS], e.top[:, :, HEADS:GR], ALU.add)
                nc.vector.tensor_scalar(e.index[:], e.code[:], float(KEYS * KEYS + KEYS), None,
                                        ALU.add).then_inc(e.indexed, 1)

            def experts_dot(e, n, t):
                dve.wait_ge(e.fetched[t], (n + 1) * (16 * HEADS))
                for h in range(HEADS):
                    row = e.rows[:, t, h, 0:P]
                    op = nc.vector.tensor_tensor_reduce(row, row, e.xn[:, t, :], 1.0, 0.0, ALU.mult, ALU.add,
                                                        e.dot[:, t, h:h + 1])
                op.then_inc(e.dotted, 1)

            def experts_weigh(e, n):
                dve.wait_ge(e.gelu, at(n, 1))
                nc.vector.scalar_tensor_tensor(out=e.coef[:], in0=e.score[:], scalar=0.0, in1=e.act[:], op0=ALU.max,
                                               op1=ALU.mult).then_inc(e.weighed, 1)

            def iteration(i, q, has):
                b = {p: i + o for p, o in OFFSET.items()}
                def spread_tile(w, n):
                    return bcast[SPREAD.index((w, n)) % NBC][:].to_broadcast([P, NH, T])

                def feed(c, src, n):
                    if n == 0:
                        dve.wait_ge(du_done, at(c, 1))
                    dve.wait_ge(b_spread, at(c, NS, n))
                    before = [k for k in range(n) if BUFFER[k] == BUFFER[n]]
                    if before:
                        dve.wait_ge(y_sum, at(c, NS, before[-1]))
                    elif later(c):
                        dve.wait_ge(y_sum, at(c - 1, NS, max(k for k in range(NS) if BUFFER[k] == BUFFER[n])))
                    nc.vector.tensor_tensor(hp[:, BUFFER[n], :, :], src[:], spread_tile(0, n), ALU.mult).then_inc(fed, 1)

                for n in range(NS):
                    if CORE in has:
                        c = b[CORE]
                        state = hp[:, BUFFER[n], :, :]
                        flat = state.rearrange("p a b -> p (a b)")
                        dve.wait_ge(decays, at(c, NS, n))
                        dve.wait_ge(fed, at(c, NS, n))
                        nc.vector.tensor_tensor_scan(flat, dA[:, n % NDA, :, :].rearrange("p a b -> p (a b)"), flat,
                                                     0.0, ALU.mult, ALU.add).then_inc(scanned, 1)
                        if n + 1 < NS:
                            feed(c, du[q], n + 1)
                        if n in DVE_STATES:
                            dve.wait_ge(c_spread, at(c, NS, n))
                            dve.wait_ge(scanned, at(c, NS, n))
                            nc.vector.tensor_tensor(state, state, spread_tile(1, n), ALU.mult).then_inc(read_out, 1)
                    for m, r, _ in due("dve_norm_x", i, q, n):
                        dve.wait_ge(p_rstd, at(m, 2, 1))
                        nc.vector.tensor_tensor(s20[:], rs0[:], rr0[:], ALU.mult).then_inc(p_scale, 1)
                        dve.wait_ge(p_scale, P_SCALE0 + at(m, 1))
                        if later(m):
                            dve.wait_ge(p_turned, at(m - 1, 1))
                        normalise(xr, x_in, mv0, s20, p_normed)
                    for m, r, t in due("dve_dot_e1", i, q, n):
                        experts_dot(e1, m, t)
                    for m, r, t in due("dve_dot_e2", i, q, n):
                        experts_dot(e2, m, t)
                    for m, r, _ in due("dve_stats_c", i, q, n):
                        dve.wait_ge(b_z, at(m, 1))
                        statistics(tokens(2), stC, mvC, c_stats, at(m, 2, 0))
                    for m, r, _ in due("dve_offset_c", i, q, n):
                        dve.wait_ge(c_rstd, at(m, 1))
                        negative_mean(offC, mvC, rsC, c_offset)
                    for m, r, _ in due("dve_stats_e2", i, q, n):
                        dve.wait_ge(x3_done, at(m, 1))
                        statistics(x3[r], e2.st, e2.mv, e2.stats, at(m, 2, 0))
                    for m, r, _ in due("dve_norm_e2", i, q, n):
                        dve.wait_ge(e2.rstd, at(m, 1))
                        normalise(e2.xn, x3[r], e2.mv, e2.rs, e2.normed)
                    for m, r, t in due("dve_top_e2", i, q, n):
                        if t == 0:
                            dve.wait_ge(e1.picks, at(min(m + 2, NB - 1) if isinstance(m, int) else m + 2, 3, 1))
                        experts_top(e2, 0, m, t)
                    for m, r, _ in due("dve_index_e2", i, q, n):
                        experts_index(e2, m)
                    for m, r, _ in due("dve_stats_a", i, q, n):
                        dve.wait_ge(a_z, at(m, 1))
                        statistics(tokens(1), stA, mvA, a_stats, at(m, 2, 0))
                    for m, r, _ in due("dve_offset_a", i, q, n):
                        dve.wait_ge(a_rstd, at(m, 1))
                        negative_mean(offA, mvA, rsA, a_offset)
                    for m, r, _ in due("dve_stats_e1", i, q, n):
                        dve.wait_ge(x1_done, at(m, 1))
                        statistics(x1[r], e1.st, e1.mv, e1.stats, at(m, 2, 0))
                    for m, r, _ in due("dve_norm_e1", i, q, n):
                        dve.wait_ge(e1.rstd, at(m, 1))
                        normalise(e1.xn, x1[r], e1.mv, e1.rs, e1.normed)
                    for m, r, t in due("dve_top_e1", i, q, n):
                        if t == 0 and (not isinstance(m, int) or m >= 3):
                            dve.wait_ge(e2.picks, at(m - 3, 3, 1))
                        experts_top(e1, 1, m, t)
                    for m, r, _ in due("dve_index_e1", i, q, n):
                        experts_index(e1, m)
                    for m, r, _ in due("dve_stats_x", i, q, n):
                        dve.wait_ge(x_loaded, (m + 1) * 16)
                        if later(m):
                            dve.wait_ge(p_kept, at(m - 1, 1))
                        statistics(x_in, st0, mv0, p_stats, at(m, 2, 0))
                    for m, r, _ in due("dve_square_x", i, q, n):
                        dve.wait_ge(p_rstd, at(m, 2, 0))
                        nc.vector.tensor_tensor(m20[:], mv0[:, :, 1], rs0[:], ALU.mult).then_inc(p_square, 1)
                        negative_mean(off0, mv0, rs0, p_offset)
                        dve.wait_ge(p_square, at(m, 2, 0))
                        nc.vector.tensor_tensor(m20[:], m20[:], rs0[:], ALU.mult).then_inc(p_square, 1)
                    for m, r, _ in due("dve_weigh_e1", i, q, n):
                        experts_weigh(e1, m)
                    for m, r, _ in due("dve_stats_b", i, q, n):
                        dve.wait_ge(e1.added, at(m, 1))
                        statistics(x2, stB, mvB, b_stats, at(m, 2, 0))
                    for m, r, _ in due("dve_norm_b", i, q, n):
                        dve.wait_ge(b_rstd, at(m, 1))
                        if later(m):
                            dve.wait_ge(x3_done, at(m - 1, 1))
                        normalise(xnb, x2, mvB, rsB, b_normed)
                    for m, r, _ in due("dve_scan_b", i, q, n):
                        dve.wait_ge(b_gate_sb, at(m, 1))
                        nc.vector.scalar_tensor_tensor(out=gates[IG:IG + NS, :], in0=bank[2][BX:BX + NS, :],
                                                       scalar=b_bx[0:NS, 0:1], in1=gates[IG:IG + NS, :],
                                                       op0=ALU.add, op1=ALU.mult).then_inc(b_fed, 1)
                        dve.wait_ge(b_fed, at(m, 1))
                        nc.vector.tensor_tensor_scan(gates[IG:IG + NS, :], gates[FG:FG + NS, :], gates[IG:IG + NS, :],
                                                     0.0, ALU.mult, ALU.add).then_inc(b_scanned, 1)
                    for m, r, _ in due("dve_weigh_e2", i, q, n):
                        experts_weigh(e2, m)
                if PRE in has:
                    feed(b[PRE], du[1 - q], 0)
                if CORE in has:
                    c = b[CORE]
                    dve.wait_ge(y_sum, at(c, NS, NS - 1))
                    nc.vector.tensor_tensor(ucs[q][:, 0:NH, :], ysum[:], ucs[q][:, NH:2 * NH, :],
                                            ALU.mult).then_inc(y_gated, 1)

            run_pipeline(dve, iteration)

        @block.gpsimd
        def _(pool):
            def fetch(e, n, t):
                if t == 0:
                    pool.wait_ge(e.indexed, at(n, 1))
                    if later(n):
                        pool.wait_ge(e.summed, at(n - 1, 1))
                        pool.wait_ge(e.started, at(n - 1, 1))
                    pool.tensor_tensor(e.mark[:], eps[:], eps[:], ALU.add).then_inc(e.started, 1)
                for h in range(HEADS):
                    pool.indirect_dma_start(
                        e.rows[:, t, h, :], None, A["experts"],
                        bass.IndirectOffsetOnAxis(ap=e.index[:, t, h:h + 1], axis=0)).then_inc(e.fetched[t], 16)

            def affine(rows, scale, shift, s, n):
                pool.tensor_tensor(rows, rows, scale[:].unsqueeze(1).to_broadcast([P, NT, P]),
                                   ALU.mult).then_inc(s, 1)
                pool.wait_ge(s, at(n, 2, 0))
                pool.tensor_tensor(rows, rows, shift[:].unsqueeze(1).to_broadcast([P, NT, P]),
                                   ALU.add).then_inc(s, 1)
                pool.wait_ge(s, at(n, 2, 1))

            def iteration(i, q, has):
                b = {p: i + o for p, o in OFFSET.items()}
                for n in range(NS):
                    if CORE in has and n in POOL_STATES:
                        c, k = b[CORE], POOL_STATES.index(n)
                        pool.wait_ge(scanned, at(c, NS, n))
                        pool.wait_ge(c_kept, at(c, len(POOL_STATES), k))
                        state = hp[:, BUFFER[n], :, :]
                        pool.tensor_tensor(state, state,
                                           c_row[:, k % NCR, :].unsqueeze(1).to_broadcast([P, NH, T]),
                                           ALU.mult).then_inc(pool_read, 1)
                    for m, r, _ in due("pool_x1", i, q, n):
                        z = outT[:].rearrange("p (t d) -> p t d", t=NT)
                        pool.wait_ge(xres_loaded, (m + 1) * 16)
                        pool.wait_ge(a_normed, at(m, 1))
                        affine(z, ln_w, ln_b, a_affine, m)
                        if second(m):
                            pool.wait_ge(e1.added, at(m - 2, 1))
                        pool.tensor_tensor(x1[r][:], z, x_res[:].rearrange("p (t d) -> p t d", t=NT),
                                           ALU.add).then_inc(x1_done, 1)
                    for m, r, _ in due("pool_x3", i, q, n):
                        pool.wait_ge(c_normed, at(m, 1))
                        affine(xnb[:], gamma, beta, b_affine, m)
                        if second(m):
                            pool.wait_ge(stored, (m - 1) * 16)
                        pool.tensor_tensor(x3[r][:], xnb[:], x2[:], ALU.add).then_inc(x3_done, 1)
                    for m, r, _ in due("pool_rest", i, q, n):
                        if second(m):
                            pool.wait_ge(a_z, at(m - 2, 1))
                        pool.wait_ge(dbl_sb, at(m, 1))
                        pool.tensor_tensor(rest[:], dbl[:], split[r][:], ALU.subtract).then_inc(rest1, 1)
                        pool.wait_ge(part2, at(m, 1))
                        pool.tensor_tensor(rest[:], rest[:], split[r][:], ALU.subtract).then_inc(rest2, 1)
                    for m, r, _ in due("pool_delta", i, q, n):
                        pool.wait_ge(dt_log, at(m, 1))
                        pool.tensor_tensor(delta[r][:], delta[r][:], soft[:], ALU.add).then_inc(delta_done, 1)
                        pool.wait_ge(delta_done, at(m, 1))
                        if second(m):
                            pool.wait_ge(fed, at(m - 2, NS, NS - 1))
                        pool.tensor_tensor(du[r][:], delta[r][:], ucs[r][:, 0:NH, :], ALU.mult).then_inc(du_done, 1)
                    for m, r, t in due("pool_fetch_e2", i, q, n):
                        fetch(e2, m, t)
                    for m, r, t in due("pool_fetch_e1", i, q, n):
                        fetch(e1, m, t)

            run_pipeline(pool, iteration)


def kernel(**inputs):
    import numpy as np
    import concourse.bacc as bacc
    from concourse.bass_utils import run_bass_kernel_spmd

    def a(name):
        return np.asarray(inputs["L0_attn_a_" + name])

    def b(name):
        return np.asarray(inputs["L0_attn_b_" + name])

    def f(name):
        return np.asarray(inputs["L0_ffn_" + name])

    def halves(v):
        return v.reshape(NH, P, -1).transpose(1, 0, 2)

    data = {
        "x": a("x"),
        "in_proj_t": a("in_proj_w").T,
        "taps": a("conv_w").T.reshape(NK * DI),
        "norm_w": a("norm_w")[:, None],
        "conv_b": halves(a("conv_b"))[:, :, 0],
        "xproj_t": halves(a("x_proj_w").T),
        "dt_w_t": a("dt_w").T,
        "dt_b": halves(a("dt_b"))[:, :, 0],
        "A_log": halves(a("A_log")),
        "Dp": halves(a("Dp"))[:, :, 0],
        "out_t": halves(a("out_proj_w").T),
        "ff1_t": a("ff_w1").T, "b1": a("ff_b1")[:, None],
        "ff2_t": a("ff_w2").T, "b2": a("ff_b2")[:, None],
        "ln_w": a("ff_ln_w"), "ln_b": a("ff_ln_b"),
        "W_in": b("W_in"), "b_in": b("b_in")[:, None],
        "wb_t": b("W_B").T, "b_B": b("b_B")[:, None], "B_mat": b("B_mat"), "C_mat": b("C_mat"),
        "W_D": b("W_D"), "b_D": b("b_D")[:, None], "W_out": b("W_out"), "b_out": b("b_out")[:, None],
        "W_ig": b("W_ig"), "b_ig": b("b_ig")[:, None], "W_fg": b("W_fg"), "b_fg": b("b_fg")[:, None],
        "gamma": b("gamma"), "beta": b("beta"),
        "wq_t": f("w_q").T.reshape(GR, DK, P).transpose(1, 0, 2),
        "key_t": f("keys").transpose(3, 2, 0, 1).reshape(DK, GR, KEYS),
        "experts": np.concatenate([f("w_down"), f("w_up")], axis=1),
    }
    data = {k: np.ascontiguousarray(v) for k, v in data.items()}

    nc = bacc.Bacc("TRN2", target_bir_lowering=False, num_devices=1)
    tensors = {k: nc.dram_tensor("in_" + k, v.shape, mybir.dt.from_np(v.dtype), kind="ExternalInput").ap()
               for k, v in data.items()}
    tensors["x"] = tensors["x"].rearrange("b (t p) d -> b p t d", p=P)
    y = nc.dram_tensor("y", (NB, T, P), F32, kind="ExternalOutput").ap()
    tensors["y"] = y.rearrange("b (t p) d -> b p t d", p=P)
    build(nc, tensors)
    return run_bass_kernel_spmd(nc, [{"in_" + k: v for k, v in data.items()}], core_ids=[0]).results[0]["y"]
```
